# Optimizing a Trainium2 kernel written in Bass

```python
import numpy as np
import jax
import jax.numpy as jnp

def _softmax(x, axis=-1):
    return jax.nn.softmax(x, axis=axis)

def _gelu(x):
    return jax.nn.gelu(x, approximate=True)

def _silu(x):
    return jax.nn.silu(x)

def _sigmoid(x):
    return jax.nn.sigmoid(x)

def _layernorm(x, axis=-1, eps=1e-05):
    m = jnp.mean(x, axis=axis, keepdims=True)
    v = jnp.var(x, axis=axis, keepdims=True)
    return (x - m) / jnp.sqrt(v + eps)

def _scatter_add(tgt, idx, src, axis=0):
    return tgt.at[idx].add(src)

def _segment_sum(src, seg, n):
    return jax.ops.segment_sum(src, seg, n)
kernel_name = 'mk_adj_ffn_d2_adj_r2_2837a0'

def setup_inputs(seed: int=0):
    np.random.seed(seed)
    _w = jnp.asarray

    def _rec_inputs():
        import jax
        import jax.numpy as jnp
        _gk = jax.random.key(seed)
        x = -0.0002928 + 1 * jax.random.normal(jax.random.fold_in(_gk, 1), (128, 128, 128), jnp.float32)
        _a = jax.random.bernoulli(jax.random.fold_in(_gk, 2), 0.03125, (128, 128))
        _a = jnp.logical_or(_a, jnp.swapaxes(_a, -1, -2))
        _a = jnp.logical_or(_a, jnp.eye(128, dtype=bool))
        adj = _a.astype(jnp.int32)
        return (x, adj)
    x, adj = _rec_inputs()

    def _L0_gnn_setup():
        import jax, jax.numpy as jnp
        import numpy as np
        NEG_BIG = -9000000000000000.0
        key = jax.random.key(seed)
        k1, k2, k3, k4 = jax.random.split(key, 4)
        bs, N, Fin, Fout = (8, 1024, 128, 128)
        x = jax.random.normal(k1, (bs, N, Fin), dtype=jnp.float32)
        adj = jax.random.randint(k2, (N, N), 0, 2, dtype=jnp.int32)
        W = jax.random.normal(k3, (Fin, Fout), dtype=jnp.float32) * (1.414 / np.sqrt(Fin))
        a = jax.random.normal(k4, (2 * Fout, 1), dtype=jnp.float32) * 0.1
        return {'x': x, 'adj': adj, 'W': W, 'a': a}
    _L0_gnn_all = _L0_gnn_setup()
    _L0_gnn_in = {k: v for k, v in _L0_gnn_all.items() if k in ('W', 'a')}
    del _L0_gnn_all

    def _L0_ffn_setup():
        import jax, jax.numpy as jnp
        import numpy as np
        D_MODEL = 128
        EXPERT_DIM = 256
        NUM_EXPERTS = 8
        TOP_K = 2
        SEQ_LEN = 1024
        BATCH = 2
        key = jax.random.key(seed)
        ks = jax.random.split(key, 8)
        s = 0.02
        x = jax.random.normal(ks[0], (SEQ_LEN, BATCH, D_MODEL), dtype=jnp.float32)
        Wg = jax.random.normal(ks[1], (D_MODEL, NUM_EXPERTS), dtype=jnp.float32) * s
        bg = jax.random.normal(ks[2], (NUM_EXPERTS,), dtype=jnp.float32) * s
        bias = jnp.zeros((NUM_EXPERTS,), dtype=jnp.float32)
        W1 = jax.random.normal(ks[3], (NUM_EXPERTS, D_MODEL, EXPERT_DIM), dtype=jnp.float32) * s
        b1 = jax.random.normal(ks[4], (NUM_EXPERTS, EXPERT_DIM), dtype=jnp.float32) * s
        W2 = jax.random.normal(ks[5], (NUM_EXPERTS, EXPERT_DIM, D_MODEL), dtype=jnp.float32) * s
        b2 = jax.random.normal(ks[6], (NUM_EXPERTS, D_MODEL), dtype=jnp.float32) * s
        return {'x': x, 'Wg': Wg, 'bg': bg, 'bias': bias, 'W1': W1, 'b1': b1, 'W2': W2, 'b2': b2}
    _L0_ffn_all = _L0_ffn_setup()
    _L0_ffn_in = {k: v for k, v in _L0_ffn_all.items() if k in ('Wg', 'bg', 'bias', 'W1', 'b1', 'W2', 'b2')}
    del _L0_ffn_all

    def _L1_gnn_setup():
        import jax, jax.numpy as jnp
        import numpy as np
        ALPHA = 0.2
        MASK_VAL = -9000000000000000.0
        key = jax.random.key(seed)
        k1, k2, k3, k4 = jax.random.split(key, 4)
        B, N, F = (8, 512, 128)
        H, OUT = (4, 128)
        hs = OUT // H
        x = jax.random.normal(k1, (B, N, F), dtype=jnp.float32)
        adj = jax.random.randint(k2, (N, N), 0, 2, dtype=jnp.int32)
        wb = float(np.sqrt(6.0 / (F + hs)))
        ab = float(np.sqrt(6.0 / (H + 2 * hs)))
        W = jax.random.uniform(k3, (H, F, hs), dtype=jnp.float32, minval=-wb, maxval=wb)
        a = jax.random.uniform(k4, (H, 2 * hs), dtype=jnp.float32, minval=-ab, maxval=ab)
        return {'x': x, 'adj': adj, 'W': W, 'a': a}
    _L1_gnn_all = _L1_gnn_setup()
    _L1_gnn_in = {k: v for k, v in _L1_gnn_all.items() if k in ('W', 'a')}
    del _L1_gnn_all

    def _L1_ffn_setup():
        import jax, jax.numpy as jnp
        import numpy as np
        B, T, D, H, E = (16, 2048, 128, 256, 8)
        key = jax.random.key(seed)
        ks = jax.random.split(key, 5)
        x = jax.random.normal(ks[0], (B, T, D), dtype=jnp.float32)
        gate_w = jax.random.normal(ks[1], (D, E), dtype=jnp.float32) * 0.02
        gate_b = jnp.zeros((E,), dtype=jnp.float32)
        W1 = jax.random.normal(ks[2], (E, D, H), dtype=jnp.float32) * 0.02
        b1 = jnp.zeros((E, H), dtype=jnp.float32)
        W2 = jax.random.normal(ks[3], (E, H, D), dtype=jnp.float32) * 0.02
        b2 = jnp.zeros((E, D), dtype=jnp.float32)
        return {'x': x, 'gate_w': gate_w, 'gate_b': gate_b, 'W1': W1, 'b1': b1, 'W2': W2, 'b2': b2}
    _L1_ffn_all = _L1_ffn_setup()
    _L1_ffn_in = {k: v for k, v in _L1_ffn_all.items() if k in ('gate_w', 'gate_b', 'W1', 'b1', 'W2', 'b2')}
    del _L1_ffn_all
    return {'x': x, 'adj': adj, 'L0_gnn_W': _L0_gnn_in['W'], 'L0_gnn_a': _L0_gnn_in['a'], 'L0_ffn_Wg': _L0_ffn_in['Wg'], 'L0_ffn_bg': _L0_ffn_in['bg'], 'L0_ffn_bias': _L0_ffn_in['bias'], 'L0_ffn_W1': _L0_ffn_in['W1'], 'L0_ffn_b1': _L0_ffn_in['b1'], 'L0_ffn_W2': _L0_ffn_in['W2'], 'L0_ffn_b2': _L0_ffn_in['b2'], 'L1_gnn_W': _L1_gnn_in['W'], 'L1_gnn_a': _L1_gnn_in['a'], 'L1_ffn_gate_w': _L1_ffn_in['gate_w'], 'L1_ffn_gate_b': _L1_ffn_in['gate_b'], 'L1_ffn_W1': _L1_ffn_in['W1'], 'L1_ffn_b1': _L1_ffn_in['b1'], 'L1_ffn_W2': _L1_ffn_in['W2'], 'L1_ffn_b2': _L1_ffn_in['b2']}

def reference(x, adj, L0_gnn_W, L0_gnn_a, L0_ffn_Wg, L0_ffn_bg, L0_ffn_bias, L0_ffn_W1, L0_ffn_b1, L0_ffn_W2, L0_ffn_b2, L1_gnn_W, L1_gnn_a, L1_ffn_gate_w, L1_ffn_gate_b, L1_ffn_W1, L1_ffn_b1, L1_ffn_W2, L1_ffn_b2):
    import jax
    import jax.numpy as jnp

    def _L0_gnn_ref(x, adj, W, a):
        import jax, jax.numpy as jnp
        import numpy as np
        NEG_BIG = -9000000000000000.0
        alpha = 0.2
        h = jnp.matmul(x, W)
        Fout = h.shape[-1]
        a1, a2 = (a[:Fout, 0], a[Fout:, 0])
        s1 = jnp.einsum('bnf,f->bn', h, a1)
        s2 = jnp.einsum('bnf,f->bn', h, a2)
        e = jax.nn.leaky_relu(s1[:, :, None] + s2[:, None, :], negative_slope=alpha)
        attention = jnp.where(adj[None, :, :] > 0, e, NEG_BIG)
        attention = jax.nn.softmax(attention, axis=-1)
        h_prime = jnp.matmul(attention, h)
        return jax.nn.elu(h_prime)

    def _L0_ffn_ref(x, Wg, bg, bias, W1, b1, W2, b2):
        import jax, jax.numpy as jnp
        import numpy as np
        D_MODEL = 128
        EXPERT_DIM = 256
        NUM_EXPERTS = 8
        TOP_K = 2
        SEQ_LEN = 1024
        BATCH = 2
        x_flat = x.reshape(-1, D_MODEL)
        gate_logits = x_flat @ Wg + bg + bias
        topk_vals, topk_idx = jax.lax.top_k(gate_logits, TOP_K)
        topk_w = jax.nn.softmax(topk_vals, axis=-1)
        combine = (jax.nn.one_hot(topk_idx, NUM_EXPERTS, dtype=x.dtype) * topk_w[..., None]).sum(axis=1)
        h = jax.nn.relu(jnp.einsum('td,edh->teh', x_flat, W1) + b1)
        y = jnp.einsum('teh,ehd->ted', h, W2) + b2
        out = jnp.einsum('ted,te->td', y, combine)
        return out.reshape(x.shape)

    def _L1_gnn_ref(x, adj, W, a):
        import jax, jax.numpy as jnp
        import numpy as np
        ALPHA = 0.2
        MASK_VAL = -9000000000000000.0
        B, N, _ = x.shape
        H, _, hs = W.shape
        Wh = jnp.einsum('bnf,hfd->bhnd', x, W)
        a1, a2 = (a[:, :hs], a[:, hs:])
        ei = jnp.einsum('bhnd,hd->bhn', Wh, a1)
        ej = jnp.einsum('bhnd,hd->bhn', Wh, a2)
        e = ei[:, :, :, None] + ej[:, :, None, :]
        e = jnp.where(e > 0, e, ALPHA * e)
        e = jnp.where(adj[None, None] > 0, e, MASK_VAL)
        att = jax.nn.softmax(e, axis=-1)
        h = jnp.einsum('bhij,bhjd->bhid', att, Wh)
        h = h.transpose(0, 2, 1, 3).reshape(B, N, H * hs)
        return jax.nn.elu(h)

    def _L1_ffn_ref(x, gate_w, gate_b, W1, b1, W2, b2):
        import jax, jax.numpy as jnp
        import numpy as np
        B, T, D, H, E = (16, 2048, 128, 256, 8)
        Bb, Tt, Dd = x.shape
        Ee = gate_w.shape[1]
        xf = x.reshape(-1, Dd)
        N = xf.shape[0]
        logits = xf @ gate_w + gate_b
        probs = jax.nn.softmax(logits, axis=-1)
        top2_vals, top2_idx = jax.lax.top_k(probs, 2)
        cw = jnp.zeros((N, Ee), dtype=xf.dtype).at[jnp.arange(N)[:, None], top2_idx].add(top2_vals)

        def step(acc, params):
            w1, bb1, w2, bb2, we = params
            h = jax.nn.gelu(xf @ w1 + bb1, approximate=False)
            y = h @ w2 + bb2
            return (acc + we[:, None] * y, None)
        out, _ = jax.lax.scan(step, jnp.zeros_like(xf), (W1, b1, W2, b2, cw.T))
        return out.reshape(Bb, Tt, Dd)
    x = x + _L0_gnn_ref(_layernorm(x, axis=-1), adj, L0_gnn_W, L0_gnn_a)
    x = x + _L0_ffn_ref(_layernorm(x, axis=-1), L0_ffn_Wg, L0_ffn_bg, L0_ffn_bias, L0_ffn_W1, L0_ffn_b1, L0_ffn_W2, L0_ffn_b2)
    x = x + _L1_gnn_ref(_layernorm(x, axis=-1), adj, L1_gnn_W, L1_gnn_a)
    x = x + _L1_ffn_ref(_layernorm(x, axis=-1), L1_ffn_gate_w, L1_ffn_gate_b, L1_ffn_W1, L1_ffn_b1, L1_ffn_W2, L1_ffn_b2)
    return x

_drawn_inputs = setup_inputs


def setup_inputs(seed=0):
    import zlib

    import numpy as np

    out = dict(_drawn_inputs(seed))
    spreads = {'L0_ffn_bias': (0.0, 0.307),
     'L1_ffn_gate_b': (0.0, 0.782),
     'L1_ffn_b1': (0.0, 0.8),
     'L1_ffn_b2': (0.0, 0.433)}
    factors = {'L0_ffn_bg': 8.0,
     'L0_ffn_b1': 8.0,
     'L0_ffn_b2': 4.044,
     'L1_ffn_gate_w': 3.319,
     'L1_ffn_W1': 8.0,
     'L1_ffn_W2': 7.519}
    for name, (base, spread) in spreads.items():
        noise = np.random.default_rng([zlib.crc32(name.encode()), seed]).standard_normal(out[name].shape)
        drawn = base * np.exp(spread * noise) if base else spread * noise
        out[name] = jnp.asarray(drawn.astype(out[name].dtype))
    for name, factor in factors.items():
        out[name] = (out[name] * factor).astype(out[name].dtype)
    return out
```

```python
from contextlib import ExitStack

import concourse.bass as bass
from concourse import mybir

F32 = mybir.dt.float32
BF16 = mybir.dt.bfloat16
I32 = mybir.dt.int32
U32 = mybir.dt.uint32
ALU = mybir.AluOpType
ACT = mybir.ActivationFunctionType
AX_X = mybir.AxisListType.X

P = 128
QG = 4
RQ = 4
NE = 8
HID = 256
PAIRS = [(a, b) for a in range(NE) for b in range(a + 1, NE)]
NPAIR = len(PAIRS)
ROW = P + 4
PACK = 2 * HID + 2 + P // 2
EPS = 1e-5
ALPHA = 0.2
MASKED = -9.0e15
NEVER = -3.0e38


def build_program(nc, x, adj, gnn_w, gnn_a, gate_w, gate_b, w1, b1, w2, b2, consts, out):
    NG = x.shape[0]
    NQ = NG // QG
    NB = NQ // RQ
    RG = QG * RQ
    TILES = NG + NPAIR - 1
    NT = -(-TILES // 4) * 4
    CAP = NG * P + P
    HEADS = (1, gnn_w[1].shape[0])
    N_CONSTS = 7 + len(gate_b) + 2 * HEADS[1]
    ROUTE_LINKS, PLACE_LINKS, PLAN_LINKS, PACK_LINKS = 23, 3, 21, 8
    TB = 2 * P
    assert TILES <= TB and NB >= 3 and P % HEADS[1] == 0

    rows_dram = nc.dram_tensor("rows_by_pair", (NPAIR * CAP, ROW), F32).ap()
    y_dram = nc.dram_tensor("y_by_tile", (NT * P, P), F32).ap()

    with ExitStack() as ctx:
        def sb(name, shape, dt=F32):
            return ctx.enter_context(nc.sbuf_tensor(name, shape, dt))

        def sem(name):
            return ctx.enter_context(nc.semaphore(name))

        X = sb("X", [P, NG, ROW])
        ident = sb("ident", [P, P])
        identb = sb("identb", [P, P], BF16)
        onesb = sb("onesb", [P, P], BF16)
        lower = sb("lower", [P, P], BF16)
        zeros = sb("zeros", [P, ROW])
        adj_i = sb("adj_i", [P, P], I32)
        maskneg = sb("maskneg", [P, P], BF16)
        W = [sb(f"W{l}", [P, P]) for l in range(2)]
        WT = [sb(f"WT{l}", [P, P]) for l in range(2)]
        A = [sb(f"A{l}", [P, 2, HEADS[l]]) for l in range(2)]
        wa1 = [sb(f"wa1_{l}", [P, HEADS[l], P]) for l in range(2)]
        wa2 = [sb(f"wa2_{l}", [P, HEADS[l], P]) for l in range(2)]
        Wg = [sb(f"Wg{l}", [P, NE]) for l in range(2)]
        gb_in = sb("gb_in", [P, 3, NE])
        gbias = [sb(f"gbias{l}", [P, NE]) for l in range(2)]
        experts = sb("experts", [P, NE, PACK])
        b2_rows = sb("b2_rows", [3, NE * P])
        b2_part = sb("b2_part", [3, 3, NE * P], BF16)

        def two(name, shape, dt=F32):
            return [sb(f"{name}{k}", shape, dt) for k in range(2)]

        mv = two("mv", [P, QG, 2])
        mv2 = two("mv2", [P, QG, 2])
        st = sb("st", [P, QG, 6])
        st2 = sb("st2", [P, QG, 6])
        neghalf = sb("neghalf", [P, QG])
        xn = two("xn", [P, QG, P])
        xnT = two("xnT", [P, QG * P])
        hsb = two("hsb", [P, QG * P])
        nmx = two("nmx", [P, 4])
        negm = two("negm", [P, 4])
        rel = two("rel", [P, 4 * P])
        es = two("es", [P, 4 * P])
        ps = two("ps", [P, 4 * P])
        pT = two("pT", [P, 4 * P])
        rowsum = two("rowsum", [P, QG * max(HEADS)])
        rinv = sb("rinv", [P, QG * max(HEADS)])
        hp = two("hp", [P, QG * P])
        mn = two("mn", [P, QG * P])
        ex = two("ex", [P, QG * P])
        xn2 = two("xn2", [P, QG, P])
        xn2T = two("xn2T", [P, QG * P])
        yg = two("yg", [P, QG, P])
        osb = two("osb", [P, QG, P])

        lg = sb("lg", [P, RG, NE])
        m1 = sb("m1", [P, RG])
        lm = sb("lm", [P, RG, NE])
        EX = sb("EX", [P, RG, NE])
        eq = sb("eq", [P, RG, NE])
        c1 = sb("c1", [P, RG])
        oh = sb("oh", [P, RG, NE])
        l2 = sb("l2", [P, RG, NE])
        sel = sb("sel", [P, RG, NE])
        tmp8 = sb("tmp8", [P, RG, NE])
        code = sb("code", [P, RG])
        den = sb("den", [P, RG])
        cw = sb("cw", [P, RG, NE])
        cwh = sb("cwh", [P, RG, NE])
        pc = sb("pc", [P, (RG + 1) * NPAIR], BF16)
        slm = sb("slm", [P, RG, NPAIR])
        slotf = sb("slotf", [P, RG])
        base = sb("base", [P, NPAIR])
        code_all = sb("code_all", [P, NG])
        slot_all = sb("slot_all", [P, NG])
        idx_rows = [sb(f"idx_rows{l}", [P, NG], U32) for l in range(2)]
        gidx = [sb(f"gidx{l}", [P, NG], U32) for l in range(2)]
        cst = sb("cst", [P, 3 * NE + 5 * NPAIR])
        revidx, pow2, pow2x2 = (cst[:, k * NE:(k + 1) * NE] for k in range(3))
        pairconst, region, grow_region, grow_lower, grow_upper = (
            cst[:, 3 * NE + k * NPAIR:3 * NE + (k + 1) * NPAIR] for k in range(5))
        ones_pair = sb("ones_pair", [P, NPAIR])
        tile_no = sb("tile_no", [P, 2])
        cnt = sb("cnt", [P, NPAIR])
        cnt_i = sb("cnt_i", [P, NPAIR], I32)
        cnt_j = sb("cnt_j", [P, NPAIR], I32)
        wpair = sb("wpair", [P, RG, 2])
        ntile = sb("ntile", [P, NPAIR])
        cum = sb("cum", [P, NPAIR])
        shift = sb("shift", [P, NPAIR])
        le = sb("le", [P, 2, NPAIR])
        lx = sb("lx", [P, 2, NPAIR])
        tvals = sb("tvals", [P, 2, 3])
        tstart = sb("tstart", [P, 2])
        tvalid = sb("tvalid", [P, 2])
        base_i = sb("base_i", [P, NPAIR], I32)
        table = sb("table", [3, TB], I32)

        xs = [sb(f"xs{k}", [P, ROW]) for k in range(4)]
        xsn = two("xsn", [P, P])
        xsT = two("xsT", [P, P])
        wst = [sb(f"wst{k}", [P, 2, PACK]) for k in range(4)]
        hh = two("hh", [P, 4, P])
        ya = two("ya", [P, P])
        yo = [sb(f"yo{k}", [P, P]) for k in range(4)]

        bank = [ctx.enter_context(nc.psum_tensor(f"bank{k}", [P, 512], F32)) for k in range(8)]
        T_, H_, E_, PT_, O_, T2_, G_ = bank[0], bank[1], bank[2:4], bank[4], bank[5], bank[6], bank[7]
        XT_, HH_, Y_ = bank[0:2], bank[2:6], bank[6:8]

        consts_in, consts_dve, consts_pool = sem("consts_in"), sem("consts_dve"), sem("consts_pool")
        setup_pe, setup_act = sem("setup_pe"), sem("setup_act")
        experts_in, b2_in, packed = sem("experts_in"), sem("b2_in"), sem("packed")
        x_in = [sem(f"x_in{j}") for j in range(RQ)]
        gathered = [sem(f"gathered{j}") for j in range(RQ)]
        x_added = sem("x_added")
        moments, rstd, xn_ready = sem("moments"), sem("rstd"), sem("xn_ready")
        moments2, rstd2, xn2_ready = sem("moments2"), sem("rstd2"), sem("xn2_ready")
        stats_done, stats2_done, eps_added = sem("stats_done"), sem("stats2_done"), sem("eps_added")
        xT_done, xT_copied, h_done, h_copied = sem("xT_done"), sem("xT_copied"), sem("h_done"), sem("h_copied")
        s_done, max_done, negm_done = sem("s_done"), sem("max_done"), sem("negm_done")
        rel_done, e_done, p_done = sem("rel_done"), sem("e_done"), sem("p_done")
        pT_done, pT_copied, o_done = sem("pT_done"), sem("pT_copied"), sem("o_done")
        rinv_done, hp_done, mn_done, ex_done = sem("rinv_done"), sem("hp_done"), sem("mn_done"), sem("ex_done")
        pos_added, resid_done = sem("pos_added"), sem("resid_done")
        x2T_done, x2T_copied, logits_done, lg_done = sem("x2T_done"), sem("x2T_copied"), sem("logits_done"), sem("lg_done")
        route, lm_done, EX_done, pc_done = sem("route"), sem("lm_done"), sem("EX_done"), sem("pc_done")
        ranks_done, slots_done, scattered = sem("ranks_done"), sem("slots_done"), sem("scattered")
        plan, tvals_done, tableT_done, table_done = sem("plan"), sem("tvals_done"), sem("tableT_done"), sem("table_done")
        padded, absorbed = sem("padded"), sem("absorbed")
        xs_in = [sem(f"xs_in{k}") for k in range(4)]
        xsn_done, staged, xsT_done, xsT_copied = sem("xsn_done"), sem("staged"), sem("xsT_done"), sem("xsT_copied")
        hh_done, act_done, y_done, ya_done, yo_done = sem("hh_done"), sem("act_done"), sem("y_done"), sem("ya_done"), sem("yo_done")
        y_out = [sem(f"y_out{k}") for k in range(4)]
        base_reset, placing, finding = sem("base_reset"), sem("placing"), sem("finding")
        gidx_done, out_added = sem("gidx_done"), sem("out_added")
        out_stored = [sem(f"out_stored{k}") for k in range(2)]

        block = ctx.enter_context(nc.Block())

        def attention_steps(eng, step, tail):
            for t in range(2 * RQ):
                step(t, t % RQ, t // RQ)
            with eng.Fori(2, NB) as b:
                for j in range(RQ):
                    step(b * RQ + j, j, b)
            for t in range(NQ, NQ + tail):
                step(t, t % RQ, t // RQ)

        def tile_steps(eng, step, tail):
            for t in range(8):
                step(t, t % 4)
            with eng.Fori(2, NT // 4) as b:
                for j in range(4):
                    step(b * 4 + j, j)
            for t in range(NT, NT + tail):
                step(t, t % 4)

        def there(t, lag, n):
            return not isinstance(t, int) or 0 <= t - lag < n

        def since(t, back):
            return not isinstance(t, int) or t >= back

        def xcols(q, lo, hi):
            if isinstance(q, int):
                return X[:, QG * q:QG * q + QG, lo:hi]
            return X[:, bass.ds(q * QG, QG), lo:hi]

        def graph(q, g, lo, hi):
            if isinstance(q, int):
                return X[:, QG * q + g, lo:hi]
            return X[:, bass.ds(q * QG + g, 1), lo:hi].rearrange("p a d -> p (a d)")

        def of_batch(t, b):
            if isinstance(b, int):
                return t[:, RG * b:RG * b + RG]
            return t[:, bass.ds(b * RG, RG)]

        def each(t, n):
            return t.unsqueeze(2).to_broadcast([P, t.shape[1], n])

        def along(t, k):
            return t.unsqueeze(1).to_broadcast([P, k, t.shape[1]])

        @block.sync
        def _(sp):
            loads = [(adj_i[:, :], adj), (W[0][:, :], gnn_w[0]),
                     (W[1][:, :].rearrange("p (h d) -> p h d", h=HEADS[1]), gnn_w[1].rearrange("h f d -> f h d")),
                     (Wg[0][:, :], gate_w[0]), (Wg[1][:, :], gate_w[1]),
                     (A[0][:, :, :].rearrange("p c h -> p (c h)"), gnn_a[0].rearrange("(c p) h -> p (c h)", c=2)),
                     (cst[:, :], consts.partition_broadcast(P))]
            for k, v in enumerate(gate_b):
                loads.append((gb_in[:, k, :], v.partition_broadcast(P)))
            for dst, src in loads:
                sp.dma_start(dst, src, allow_slow_non_contiguous=True).then_inc(consts_in, 16)
            sp.wait_ge(consts_pool, 1)
            hs = P // HEADS[1]
            for h in range(HEADS[1]):
                for c in range(2):
                    sp.dma_start(A[1][h * hs:(h + 1) * hs, c, h:h + 1],
                                 gnn_a[1][h:h + 1, c * hs:(c + 1) * hs].rearrange("a d -> d a"),
                                 allow_slow_non_contiguous=True).then_inc(consts_in, 16)

            def load_x(t, j, B):
                if since(t, RQ):
                    sp.wait_ge(x_in[j], B * 16)
                src = x[QG * t:QG * t + QG] if isinstance(t, int) else x[bass.ds(t * QG, QG)]
                sp.dma_start(xcols(t, 0, P), src.rearrange("g p d -> p g d")).then_inc(x_in[j], 16)

            attention_steps(sp, load_x, 0)

            for l in range(2):
                if l == 0:
                    sp.wait_ge(consts_pool, 2)
                else:
                    sp.wait_ge(staged, 2 * NT)
                for e in range(NE):
                    sp.dma_start(experts[:, e, 0:HID], w1[l][e]).then_inc(experts_in, 16)
                    sp.dma_start(experts[:, e, HID:2 * HID].rearrange("p (c d) -> p c d", c=2),
                                 w2[l][e].rearrange("(c p) d -> p c d", c=2)).then_inc(experts_in, 16)
                    sp.dma_start(experts[:, e, 2 * HID:2 * HID + 2],
                                 b1[l][e].rearrange("(c p) -> p c", c=2),
                                 allow_slow_non_contiguous=True).then_inc(experts_in, 16)
                sp.dma_start(b2_rows[:, :], b2[l].rearrange("e d -> (e d)").partition_broadcast(3)).then_inc(b2_in, 16)

                sp.wait_ge(plan, (l + 1) * PLAN_LINKS)
                sp.wait_ge(scattered, 16 * NG * (l + 1))
                for c in range(NPAIR):
                    end = sp.value_load(base_i[0:1, c:c + 1], min_val=0, max_val=NPAIR * CAP - P)
                    sp.dma_start(rows_dram[bass.ds(end, P), :], zeros[:, :]).then_inc(padded, 16)
                sp.wait_ge(padded, 16 * NPAIR * (l + 1))
                sp.wait_ge(table_done, l + 1)

                def tile_io(t, j, l=l):
                    T = NT * l + t
                    if there(t, 0, NT):
                        col = slice(t, t + 1) if isinstance(t, int) else bass.ds(t, 1)
                        row = sp.value_load(table[0:1, col], min_val=0, max_val=NPAIR * CAP - P)
                    if l or since(t, 4):
                        sp.wait_ge(yo_done, T - 3)
                    if there(t, 4, NT):
                        dst = y_dram[(t - 4) * P:(t - 3) * P] if isinstance(t, int) else y_dram[bass.ds((t - 4) * P, P)]
                        sp.dma_start(dst, yo[j][:, :]).then_inc(y_out[j], 16)
                    if there(t, 0, NT):
                        sp.dma_start(xs[j][:, :], rows_dram[bass.ds(row, P), :]).then_inc(xs_in[j], 16)

                tile_steps(sp, tile_io, 4)

            with sp.Fori(0, NQ // 2) as b:
                for k in range(2):
                    sp.wait_ge(out_added, b * 2 + (k + 1))
                    sp.dma_start(out[bass.ds((b * 2 + k) * QG, QG)].rearrange("g p d -> p g d"),
                                 osb[k][:, :, :]).then_inc(out_stored[k], 16)
            for k in range(2):
                sp.wait_ge(out_stored[k], 16 * (NQ // 2))

        @block.gpsimd
        def _(pool):
            pool.memset(A[1][:, :, :], 0.0).then_inc(consts_pool, 1)
            pool.memset(experts[:, :, 2 * HID + 2:PACK], 0.0).then_inc(consts_pool, 1)
            pool.memset(onesb[:, :], 1.0)
            pool.memset(zeros[:, :], 0.0)
            pool.memset(ones_pair[:, :], 1.0)
            pool.memset(neghalf[:, :], -0.5)
            pool.memset(pc[:, :], 0.0)
            pool.iota(tile_no[:, :], [[P, 2]], base=0, channel_multiplier=1, allow_small_or_imprecise_dtypes=True)
            pool.memset(lower[:, :], 0.0)
            pool.memset(identb[:, :], 0.0)
            pool.memset(ident[:, :], 0.0).then_inc(consts_pool, 1)
            pool.wait_ge(consts_pool, 3)
            pool.affine_select(out=ident[:, :], in_=ident[:, :], compare_op=ALU.not_equal, fill=1.0, base=0,
                               pattern=[[-1, P]], channel_multiplier=1)
            pool.affine_select(out=identb[:, :], in_=identb[:, :], compare_op=ALU.not_equal, fill=1.0, base=0,
                               pattern=[[-1, P]], channel_multiplier=1)
            pool.affine_select(out=lower[:, :], in_=lower[:, :], compare_op=ALU.is_ge, fill=1.0, base=0,
                               pattern=[[-1, P]], channel_multiplier=1).then_inc(consts_pool, 1)

            n_eps = [0]

            def deviation(m, done, ready, n):
                pool.wait_ge(done, n)
                pool.tensor_scalar(m[:, :, 1], m[:, :, 1], EPS, None, ALU.add).then_inc(eps_added, 1)
                n_eps[0] += 1
                pool.wait_ge(eps_added, n_eps[0])
                pool.tensor_tensor(m[:, :, 1], m[:, :, 1], neghalf[:, :], ALU.pow).then_inc(ready, 1)

            def gather(l, q):
                if q >= 2:
                    if l == 1:
                        pool.wait_ge(x_added, q - 1)
                    else:
                        pool.wait_ge(out_added, q - 1)
                elif l == 2:
                    pool.wait_ge(x_added, NQ)
                for g in range(QG):
                    n = QG * q + g
                    pool.indirect_dma_start(yg[q % 2][:, g, :], None, y_dram,
                                            bass.IndirectOffsetOnAxis(ap=gidx[l - 1][:, n:n + 1], axis=0)
                                            ).then_inc(gathered[q % RQ], 16)

            def add(q):
                pool.wait_ge(gathered[q % RQ], 16 * QG * (q // RQ + 1))
                xq = X[:, QG * q:QG * q + QG, 0:P]
                pool.tensor_tensor(xq, xq, yg[q % 2][:, :, :], ALU.add).then_inc(x_added, 1)

            for l in range(3):
                if l:
                    for k in range(4):
                        pool.wait_ge(y_out[k], 4 * NT * l)
                    pool.wait_ge(gidx_done, NB * l)
                    gather(l, 0)
                    gather(l, 1)
                if l == 2:
                    for q in range(2, NQ):
                        gather(l, q)
                    break
                for t in range(NQ + 2 * RQ + 1):
                    if l and t < NQ:
                        add(t)
                        if t + 2 < NQ:
                            gather(l, t + 2)
                    if t < NQ:
                        deviation(mv[t % 2], moments, rstd, l * NQ + t + 1)
                    if 0 <= t - 3 < NQ:
                        deviation(mv2[(t - 3) % 2], moments2, rstd2, l * NQ + t - 3 + 1)
                    b, part = divmod(t - 9, RQ)
                    if 0 <= b < NB:
                        pool.wait_ge(slots_done, l * NB + b + 1)
                        for n in range(RG * b + QG * part, RG * b + QG * part + QG):
                            pool.indirect_dma_start(rows_dram,
                                                    bass.IndirectOffsetOnAxis(ap=idx_rows[l][:, n:n + 1], axis=0),
                                                    X[:, n, :], None).then_inc(scattered, 16)

        @block.tensor
        def _(pe):
            pe.wait_ge(consts_pool, 4)
            pe.wait_ge(consts_in, 16 * N_CONSTS)
            for l in range(2):
                mm = pe.transpose(bank[l][:, 0:P], W[l][:, :], ident[:, :])
            mm.then_inc(setup_pe, 1)
            pe.wait_ge(setup_act, 2)
            for l in range(2):
                for c in range(2):
                    mm = pe.matmul(bank[2 + 2 * l + c][:, 0:HEADS[l] * P], WT[l][:, :], each(A[l][:, c, :], P),
                                   start=True, stop=True)
            mm.then_inc(setup_pe, 1)
            pe.wait_ge(setup_act, 6)
            pe.wait_ge(consts_dve, 3)

            for l in range(2):
                H = HEADS[l]
                hs = P // H

                def transposes(t, j):
                    q = t - 1
                    if not there(t, 1, NQ):
                        return
                    G = l * NQ + q
                    k = (j - 1) % 2
                    pe.wait_ge(xn_ready, G + 1)
                    if l or since(t, 2):
                        pe.wait_ge(xT_copied, G)
                    for g in range(QG):
                        mm = pe.transpose(T_[:, g * P:(g + 1) * P], xn[k][:, g, :], ident[:, :])
                    mm.then_inc(xT_done, 1)

                def project(t, j):
                    q = t - 1
                    if not there(t, 1, NQ):
                        return
                    G = l * NQ + q
                    k = (j - 1) % 2
                    pe.wait_ge(xT_copied, G + 1)
                    if l or since(t, 2):
                        pe.wait_ge(h_copied, G)
                    for g in range(QG):
                        mm = pe.matmul(H_[:, g * P:(g + 1) * P], xnT[k][:, g * P:(g + 1) * P], W[l][:, :],
                                       start=True, stop=True)
                    mm.then_inc(h_done, 1)

                def scores(t, j, u):
                    q = t - 2
                    if not there(t, 2, NQ):
                        return
                    k = j % 2
                    n = q if l == 0 else NQ + q * QG + u
                    e = E_[k if l == 0 else u % 2]
                    if l or since(t, 4):
                        pe.wait_ge(e_done, n - 1)
                    pe.matmul(e[:, :], identb[:, :], along(maskneg[:, :], 4), start=True, stop=False)
                    if l == 0:
                        pe.matmul(e[:, :], wa2[0][:, 0, :], xnT[k][:, :], start=False, stop=False)
                        for g in range(QG):
                            mm = pe.matmul(e[:, g * P:(g + 1) * P], xnT[k][:, g * P:(g + 1) * P], wa1[0][:, 0, :],
                                           start=False, stop=(g == QG - 1))
                    else:
                        xg = xnT[k][:, u * P:(u + 1) * P]
                        pe.matmul(e[:, :], xg, wa1[1][:, :, :], start=False, stop=False)
                        for h in range(H):
                            mm = pe.matmul(e[:, h * P:(h + 1) * P], wa2[1][:, h, :], xg,
                                           start=False, stop=(h == H - 1))
                    mm.then_inc(s_done, 1)

                def turn(t, j, u):
                    q = t - 2
                    if not there(t, 2, NQ):
                        return
                    n = q if l == 0 else NQ + q * QG + u
                    k = j % 2 if l == 0 else u % 2
                    pe.wait_ge(p_done, n + 1)
                    if l or since(t, 3):
                        pe.wait_ge(pT_copied, n)
                    for i in range(4):
                        mm = pe.transpose(PT_[:, i * P:(i + 1) * P], ps[k][:, i * P:(i + 1) * P], ident[:, :])
                    mm.then_inc(pT_done, 1)

                def mix(t, j, u):
                    q = t - 2
                    if not there(t, 2, NQ):
                        return
                    G = l * NQ + q
                    n = q if l == 0 else NQ + q * QG + u
                    k = j % 2 if l == 0 else u % 2
                    pe.wait_ge(pT_copied, n + 1)
                    if u == 0:
                        pe.wait_ge(h_copied, G + 1)
                        if l or since(t, 3):
                            pe.wait_ge(hp_done, G)
                    for i in range(4):
                        p_i = pT[k][:, i * P:(i + 1) * P]
                        if l == 0:
                            mm = pe.matmul(O_[:, i * P:(i + 1) * P], p_i, hsb[j % 2][:, i * P:(i + 1) * P],
                                           start=True, stop=True)
                        else:
                            c = slice(u * P + i * hs, u * P + (i + 1) * hs)
                            mm = pe.matmul(O_[:, c], p_i, hsb[j % 2][:, c], start=True, stop=True)
                    mm.then_inc(o_done, 1)

                def transposes2(t, j):
                    q = t - 4
                    if not there(t, 4, NQ):
                        return
                    G = l * NQ + q
                    k = j % 2
                    pe.wait_ge(xn2_ready, G + 1)
                    if l or since(t, 5):
                        pe.wait_ge(x2T_copied, G)
                    for g in range(QG):
                        mm = pe.transpose(T2_[:, g * P:(g + 1) * P], xn2[k][:, g, :], ident[:, :])
                    mm.then_inc(x2T_done, 1)

                def logits(t, j, B):
                    q = t - 4
                    if not there(t, 4, NQ):
                        return
                    G = l * NQ + q
                    k = j % 2
                    pe.wait_ge(x2T_copied, G + 1)
                    if l or since(t, 5):
                        pe.wait_ge(lg_done, G)
                    if j == 1 and since(t, 9):
                        pe.wait_ge(slots_done, l * NB + B - 1)
                    for g in range(QG):
                        mm = pe.matmul(G_[:, 480 + g * NE:480 + (g + 1) * NE], xn2T[k][:, g * P:(g + 1) * P],
                                       Wg[l][:, :], start=True, stop=True)
                    mm.then_inc(logits_done, 1)

                def ranks(t, j, B):
                    if j or not since(t, 8):
                        return
                    b = B - 2
                    width = (RG + 1) * NPAIR
                    pe.wait_ge(pc_done, l * NB + b + 1)
                    pe.wait_ge(lg_done, l * NQ + (min(t - 3, NQ) if isinstance(t, int) else t - 3))
                    pe.matmul(G_[:, 0:width], lower[:, :], pc[:, :], start=True, stop=False)
                    for s in range(1, RG + 1):
                        mm = pe.matmul(G_[:, s * NPAIR:width], onesb[:, :], pc[:, 0:width - s * NPAIR],
                                       start=False, stop=(s == RG))
                    mm.then_inc(ranks_done, 1)

                def step(t, j, B):
                    if l == 0:
                        scores(t, j, 0)
                        transposes2(t, j)
                        transposes(t, j)
                        logits(t, j, B)
                        turn(t, j, 0)
                        project(t, j)
                        mix(t, j, 0)
                        ranks(t, j, B)
                    else:
                        scores(t, j, 0)
                        scores(t, j, 1)
                        transposes2(t, j)
                        transposes(t, j)
                        turn(t, j, 0)
                        scores(t, j, 2)
                        logits(t, j, B)
                        mix(t, j, 0)
                        turn(t, j, 1)
                        project(t, j)
                        scores(t, j, 3)
                        mix(t, j, 1)
                        turn(t, j, 2)
                        mix(t, j, 2)
                        turn(t, j, 3)
                        mix(t, j, 3)
                        ranks(t, j, B)

                attention_steps(pe, step, RQ + 1)

                pe.wait_ge(tvals_done, l + 1)
                for c in range(2):
                    mm = pe.transpose(T2_[0:3, c * P:(c + 1) * P], tvals[:, c, :], ident[:, :])
                mm.then_inc(tableT_done, 1)

                def tile(t, j):
                    T = NT * l + t
                    if there(t, 0, NT):
                        pe.wait_ge(xsn_done, T + 1)
                        if l or since(t, 2):
                            pe.wait_ge(xsT_copied, T - 1)
                        pe.transpose(XT_[j % 2][:, 0:P], xsn[j % 2][:, :], ident[:, :]).then_inc(xsT_done, 1)
                    if there(t, 1, NT):
                        k = (j - 1) % 4
                        pe.wait_ge(xsT_copied, T)
                        pe.wait_ge(staged, T * 2)
                        if l or since(t, 5):
                            pe.wait_ge(act_done, T - 4)
                        for c in range(4):
                            mm = pe.matmul(HH_[k][:, c * P:(c + 1) * P],
                                           wst[k][:, c // 2, (c % 2) * P:(c % 2 + 1) * P], xsT[k % 2][:, :],
                                           start=True, stop=True)
                        mm.then_inc(hh_done, 1)
                    if there(t, 2, NT):
                        k = (j - 2) % 4
                        pe.wait_ge(act_done, T - 1)
                        if l or since(t, 4):
                            pe.wait_ge(yo_done, T - 3)
                        for e in range(2):
                            y = Y_[k % 2][:, e * P:(e + 1) * P]
                            pe.matmul(y, onesb[0:3, :], wst[k][0:3, e, 2 * HID + 2:PACK].bitcast(BF16),
                                      start=True, stop=False)
                            for c in range(2):
                                mm = pe.matmul(y, hh[k % 2][:, 2 * e + c, :],
                                               wst[k][:, e, HID + c * P:HID + (c + 1) * P],
                                               start=False, stop=(c == 1))
                        mm.then_inc(y_done, 1)

                tile_steps(pe, tile, 2)

        @block.scalar
        def _(act):
            act.preload_act_table_set("exp_and_others")
            act.wait_ge(setup_pe, 1)
            for l in range(2):
                act.activation(WT[l][:, :], bank[l][:, 0:P], ACT.Copy).then_inc(setup_act, 1)
            act.wait_ge(setup_pe, 2)
            for l in range(2):
                for c, wa in enumerate((wa1, wa2)):
                    act.activation(wa[l][:, :, :].rearrange("p h d -> p (h d)"),
                                   bank[2 + 2 * l + c][:, 0:HEADS[l] * P], ACT.Copy).then_inc(setup_act, 1)

            for l in range(2):
                H = HEADS[l]

                def copy_xT(t, j):
                    if there(t, 1, NQ):
                        G = l * NQ + t - 1
                        act.wait_ge(xT_done, G + 1)
                        if l or since(t, 3):
                            act.wait_ge(s_done, s_last(l, t - 3))
                        act.activation(xnT[(j - 1) % 2][:, :], T_[:, :], ACT.Copy).then_inc(xT_copied, 1)

                def s_last(l, q):
                    return q + 1 if l == 0 else NQ + (q + 1) * QG if not isinstance(q, int) or q >= -1 else NQ

                def copy_h(t, j):
                    if there(t, 1, NQ):
                        G = l * NQ + t - 1
                        act.wait_ge(h_done, G + 1)
                        if l or since(t, 3):
                            act.wait_ge(o_done, s_last(l, t - 3))
                        act.activation(hsb[(j - 1) % 2][:, :], H_[:, :], ACT.Copy).then_inc(h_copied, 1)

                def rectify(t, j, u):
                    if there(t, 2, NQ):
                        q = t - 2
                        n = q if l == 0 else NQ + q * QG + u
                        k = j % 2 if l == 0 else u % 2
                        act.wait_ge(max_done, n + 1)
                        if l or since(t, 4):
                            act.wait_ge(e_done, n - 1)
                        act.activation(rel[k][:, :], E_[k][:, :], ACT.Relu, scale=1.0 - ALPHA).then_inc(rel_done, 1)

                def exps(t, j, u):
                    if there(t, 2, NQ):
                        q = t - 2
                        G = l * NQ + q
                        n = q if l == 0 else NQ + q * QG + u
                        k = j % 2 if l == 0 else u % 2
                        act.wait_ge(e_done, n + 1)
                        if l or since(t, 4):
                            act.wait_ge(pT_done, n - 1)
                            if u == 0:
                                act.wait_ge(rinv_done, G - 1)
                        for i in range(4):
                            ins = act.activation(ps[k][:, i * P:(i + 1) * P], es[k][:, i * P:(i + 1) * P], ACT.Exp,
                                                 bias=negm[k][:, i:i + 1],
                                                 accum_out=rowsum[j % 2][:, 4 * u + i:4 * u + i + 1])
                        ins.then_inc(p_done, 1)

                def copy_pT(t, j, u):
                    if there(t, 2, NQ):
                        q = t - 2
                        n = q if l == 0 else NQ + q * QG + u
                        k = j % 2 if l == 0 else u % 2
                        act.wait_ge(pT_done, n + 1)
                        if l or since(t, 4):
                            act.wait_ge(o_done, n - 1)
                        act.activation(pT[k][:, :], PT_[:, :], ACT.Copy).then_inc(pT_copied, 1)

                def exp_neg(t, j):
                    if there(t, 3, NQ):
                        G = l * NQ + t - 3
                        act.wait_ge(mn_done, G + 1)
                        if l or since(t, 5):
                            act.wait_ge(resid_done, G - 1)
                        act.activation(ex[(j - 3) % 2][:, :], mn[(j - 3) % 2][:, :], ACT.Exp).then_inc(ex_done, 1)

                def copy_x2T(t, j):
                    if there(t, 4, NQ):
                        G = l * NQ + t - 4
                        act.wait_ge(x2T_done, G + 1)
                        if l or since(t, 6):
                            act.wait_ge(logits_done, G - 1)
                        act.activation(xn2T[j % 2][:, :], T2_[:, :], ACT.Copy).then_inc(x2T_copied, 1)

                def exp_logits(t, j, B):
                    if j == 3 and since(t, 7) and there(t, 7, NQ):
                        act.wait_ge(lm_done, l * NB + B)
                        act.activation(EX[:, :, :], lm[:, :, :], ACT.Exp).then_inc(EX_done, 1)

                def step(t, j, B):
                    if l == 0:
                        rectify(t, j, 0)
                        copy_x2T(t, j)
                        copy_xT(t, j)
                        exps(t, j, 0)
                        copy_h(t, j)
                        exp_neg(t, j)
                        copy_pT(t, j, 0)
                        exp_logits(t, j, B)
                    else:
                        rectify(t, j, 0)
                        rectify(t, j, 1)
                        copy_x2T(t, j)
                        exps(t, j, 0)
                        copy_xT(t, j)
                        rectify(t, j, 2)
                        copy_pT(t, j, 0)
                        exps(t, j, 1)
                        copy_h(t, j)
                        rectify(t, j, 3)
                        copy_pT(t, j, 1)
                        exps(t, j, 2)
                        exp_neg(t, j)
                        copy_pT(t, j, 2)
                        exps(t, j, 3)
                        copy_pT(t, j, 3)
                        exp_logits(t, j, B)

                attention_steps(act, step, RQ)
                if l:
                    act.preload_act_table_set("gelu_and_others")
                func = ACT.Gelu if l else ACT.Relu

                def tile(t, j):
                    T = NT * l + t
                    if there(t, 0, NT):
                        act.wait_ge(xsT_done, T + 1)
                        if l or since(t, 2):
                            act.wait_ge(hh_done, T - 1)
                        act.activation(xsT[j % 2][:, :], XT_[j % 2][:, 0:P], ACT.Copy).then_inc(xsT_copied, 1)
                    if there(t, 1, NT):
                        k = (j - 1) % 4
                        act.wait_ge(hh_done, T)
                        if l or since(t, 3):
                            act.wait_ge(y_done, T - 2)
                        for c in range(4):
                            ins = act.activation(hh[k % 2][:, c, :], HH_[k][:, c * P:(c + 1) * P], func,
                                                 bias=wst[k][:, c // 2, 2 * HID + c % 2:2 * HID + c % 2 + 1])
                        ins.then_inc(act_done, 1)

                tile_steps(act, tile, 1)
                if l == 0:
                    act.preload_act_table_set("exp_and_others")

        @block.vector
        def _(dve):
            def linker(s, before, links):
                done = [0]

                def run(ins):
                    done[0] += 1
                    assert done[0] <= links
                    ins.then_inc(s, 1)
                    dve.wait_ge(s, before + done[0])
                return run

            def held(s, value):
                dve.wait_ge(s, value)
                dve.sem_inc(absorbed, 1)

            dve.wait_ge(consts_in, 16 * N_CONSTS)
            dve.tensor_scalar(maskneg[:, :], adj_i[:, :], 0, MASKED, ALU.is_le, ALU.mult).then_inc(consts_dve, 1)
            dve.tensor_tensor(gbias[0][:, :], gb_in[:, 0, :], gb_in[:, 1, :], ALU.add).then_inc(consts_dve, 1)
            dve.tensor_copy(gbias[1][:, :], gb_in[:, 2, :]).then_inc(consts_dve, 1)
            dve.wait_ge(consts_pool, 4)

            for l in range(2):
                H = HEADS[l]

                def first_moments(t, j, B):
                    if not there(t, 0, NQ):
                        return
                    G = l * NQ + t
                    if l == 0:
                        held(x_in[j], B * 16 + 16)
                    else:
                        held(x_added, t + 1)
                    if l or since(t, 2):
                        held(xn_ready, G - 1)
                    for g in range(QG):
                        dve.bn_stats(st[:, g, :], graph(t, g, 0, P)).then_inc(stats_done, 1)
                    held(stats_done, G * QG + QG)
                    for g in range(QG):
                        ins = dve.bn_aggr(mv[j % 2][:, g, :], st[:, g, :])
                    ins.then_inc(moments, 1)

                def normalise(t, j):
                    if not there(t, 1, NQ):
                        return
                    G = l * NQ + t - 1
                    k = (j - 1) % 2
                    dve.wait_ge(rstd, G + 1)
                    if l or since(t, 3):
                        dve.wait_ge(xT_done, G - 1)
                    for g in range(QG):
                        ins = dve.tensor_scalar(xn[k][:, g, :], graph(t - 1, g, 0, P), mv[k][:, g, 0:1],
                                                mv[k][:, g, 1:2], ALU.subtract, ALU.mult)
                    ins.then_inc(xn_ready, 1)

                def maxima(t, j, u):
                    if not there(t, 2, NQ):
                        return
                    q = t - 2
                    n = q if l == 0 else NQ + q * QG + u
                    k = j % 2 if l == 0 else u % 2
                    dve.wait_ge(s_done, n + 1)
                    dve.tensor_reduce(nmx[k][:, :], E_[k][:, :].rearrange("p (b c) -> p b c", b=4), AX_X, ALU.max,
                                      negate=True).then_inc(max_done, 1)
                    dve.wait_ge(max_done, n + 1)
                    if l or since(t, 4):
                        dve.wait_ge(p_done, n - 1)
                    dve.scalar_tensor_tensor(negm[k][:, :], nmx[k][:, :], ALPHA, nmx[k][:, :], ALU.mult,
                                             ALU.min).then_inc(negm_done, 1)

                def leaky(t, j, u):
                    if not there(t, 2, NQ):
                        return
                    q = t - 2
                    n = q if l == 0 else NQ + q * QG + u
                    k = j % 2 if l == 0 else u % 2
                    dve.wait_ge(rel_done, n + 1)
                    dve.scalar_tensor_tensor(es[k][:, :], E_[k][:, :], ALPHA, rel[k][:, :], ALU.mult,
                                             ALU.add).then_inc(e_done, 1)

                def weigh(t, j):
                    if not there(t, 3, NQ):
                        return
                    G = l * NQ + t - 3
                    k = (j - 3) % 2
                    n = (t - 3) + 1 if l == 0 else NQ + (t - 3) * QG + QG
                    dve.wait_ge(o_done, n)
                    dve.reciprocal(rinv[:, 0:QG * H], rowsum[k][:, 0:QG * H]).then_inc(rinv_done, 1)
                    dve.wait_ge(rinv_done, G + 1)
                    dve.tensor_tensor(hp[k][:, :].rearrange("p (b c) -> p b c", b=QG * H),
                                      O_[:, :].rearrange("p (b c) -> p b c", b=QG * H),
                                      each(rinv[:, 0:QG * H], P // H), ALU.mult).then_inc(hp_done, 1)
                    dve.wait_ge(hp_done, G + 1)
                    if l or since(t, 5):
                        dve.wait_ge(ex_done, G - 1)
                    dve.tensor_scalar(mn[k][:, :], hp[k][:, :], 0.0, None, ALU.min).then_inc(mn_done, 1)

                def residual(t, j):
                    if not there(t, 3, NQ):
                        return
                    q = t - 3
                    G = l * NQ + q
                    k = (j - 3) % 2
                    h3 = hp[k][:, :].rearrange("p (g d) -> p g d", g=QG)
                    dve.wait_ge(mn_done, G + 1)
                    dve.scalar_tensor_tensor(h3, h3, 0.0, xcols(q, 0, P), ALU.max, ALU.add).then_inc(pos_added, 1)
                    dve.wait_ge(pos_added, G + 1)
                    dve.wait_ge(ex_done, G + 1)
                    dve.scalar_tensor_tensor(xcols(q, 0, P), ex[k][:, :].rearrange("p (g d) -> p g d", g=QG), -1.0,
                                             h3, ALU.add, ALU.add).then_inc(resid_done, 1)
                    held(resid_done, G + 1)
                    if l or since(t, 5):
                        held(xn2_ready, G - 1)
                    for g in range(QG):
                        dve.bn_stats(st2[:, g, :], graph(q, g, 0, P)).then_inc(stats2_done, 1)
                    held(stats2_done, G * QG + QG)
                    for g in range(QG):
                        ins = dve.bn_aggr(mv2[k][:, g, :], st2[:, g, :])
                    ins.then_inc(moments2, 1)

                def normalise2(t, j):
                    if not there(t, 4, NQ):
                        return
                    q = t - 4
                    G = l * NQ + q
                    k = j % 2
                    dve.wait_ge(rstd2, G + 1)
                    if l or since(t, 6):
                        dve.wait_ge(x2T_done, G - 1)
                    dve.tensor_scalar(xcols(q, P, P + 2), mv2[k][:, :, :], 1.0, None, ALU.mult)
                    for g in range(QG):
                        ins = dve.tensor_scalar(xn2[k][:, g, :], graph(q, g, 0, P), mv2[k][:, g, 0:1],
                                                mv2[k][:, g, 1:2], ALU.subtract, ALU.mult)
                    ins.then_inc(xn2_ready, 1)

                def take_logits(t, j):
                    if not there(t, 4, NQ):
                        return
                    G = l * NQ + t - 4
                    dve.wait_ge(logits_done, G + 1)
                    dve.tensor_tensor(lg[:, QG * j:QG * j + QG, :],
                                      G_[:, 480:480 + QG * NE].rearrange("p (g e) -> p g e", g=QG),
                                      along(gbias[l][:, :], QG), ALU.add).then_inc(lg_done, 1)

                def choose(t, j, B):
                    if j != 3 or not since(t, 7) or not there(t, 7, NQ):
                        return
                    N = l * NB + B - 1
                    b = B - 1
                    link = linker(route, N * ROUTE_LINKS, ROUTE_LINKS)
                    V = dve
                    V.wait_ge(lg_done, (N + 1) * RQ)
                    link(V.tensor_reduce(m1[:, :], lg[:, :, :], AX_X, ALU.max))
                    V.tensor_tensor(lm[:, :, :], lg[:, :, :], each(m1[:, :], NE), ALU.subtract).then_inc(lm_done, 1)

                    def first_of(values, peak, onehot):
                        link(V.tensor_tensor(eq[:, :, :], values, each(peak, NE), ALU.is_equal))
                        link(V.tensor_tensor(eq[:, :, :], eq[:, :, :], along(revidx, RG), ALU.mult))
                        link(V.tensor_reduce(c1[:, :], eq[:, :, :], AX_X, ALU.max))
                        link(V.tensor_tensor(onehot, eq[:, :, :], each(c1[:, :], NE), ALU.is_equal))

                    first_of(lg[:, :, :], m1[:, :], oh[:, :, :])
                    link(V.scalar_tensor_tensor(l2[:, :, :], oh[:, :, :], NEVER, lg[:, :, :], ALU.mult, ALU.add))
                    link(V.tensor_reduce(m1[:, :], l2[:, :, :], AX_X, ALU.max))
                    first_of(l2[:, :, :], m1[:, :], sel[:, :, :])
                    link(V.tensor_tensor(sel[:, :, :], sel[:, :, :], oh[:, :, :], ALU.add))
                    link(V.tensor_tensor(tmp8[:, :, :], sel[:, :, :], along(pow2, RG), ALU.mult))
                    link(V.tensor_reduce(code[:, :], tmp8[:, :, :], AX_X, ALU.add))
                    if N_first(t):
                        V.wait_ge(ranks_done, N)
                    V.tensor_tensor(pc[:, 0:RG * NPAIR].rearrange("p (g c) -> p g c", g=RG), along(pairconst, RG),
                                    each(code[:, :], NPAIR), ALU.is_equal).then_inc(pc_done, 1)
                    V.tensor_scalar(of_batch(code_all, b), code[:, :], 1.0, None, ALU.mult)
                    V.wait_ge(EX_done, N + 1)
                    link(V.tensor_tensor(tmp8[:, :, :], sel[:, :, :], EX[:, :, :], ALU.mult))
                    link(V.tensor_reduce(den[:, :], (EX if l else tmp8)[:, :, :], AX_X, ALU.add))
                    link(V.reciprocal(den[:, :], den[:, :]))
                    link(V.tensor_tensor(cw[:, :, :], tmp8[:, :, :], each(den[:, :], NE), ALU.mult))
                    link(V.tensor_tensor(cwh[:, :, :], along(pow2x2, RG), each(code[:, :], NE), ALU.is_gt))
                    link(V.tensor_tensor(cwh[:, :, :], cwh[:, :, :], cw[:, :, :], ALU.mult))
                    link(V.tensor_reduce(wpair[:, :, 1], cwh[:, :, :], AX_X, ALU.add))
                    link(V.tensor_tensor(cw[:, :, :], cw[:, :, :], cwh[:, :, :], ALU.subtract))
                    link(V.tensor_reduce(wpair[:, :, 0], cw[:, :, :], AX_X, ALU.add))
                    V.tensor_scalar(xcols_of_batch(b, P + 2, P + 4), wpair[:, :, :], 1.0, None, ALU.mult)

                def N_first(t):
                    return l or since(t, 8)

                def xcols_of_batch(b, lo, hi):
                    if isinstance(b, int):
                        return X[:, RG * b:RG * b + RG, lo:hi]
                    return X[:, bass.ds(b * RG, RG), lo:hi]

                def place(t, j, B):
                    if j or not since(t, 8):
                        return
                    b = B - 2
                    N = l * NB + b
                    link = linker(placing, N * PLACE_LINKS, PLACE_LINKS)
                    dve.wait_ge(ranks_done, N + 1)
                    ranks = G_[:, 0:RG * NPAIR].rearrange("p (g c) -> p g c", g=RG)
                    link(dve.tensor_tensor(slm[:, :, :], ranks, along(base[:, :], RG), ALU.add))
                    link(dve.tensor_tensor(slm[:, :, :], slm[:, :, :],
                                           pc[:, 0:RG * NPAIR].rearrange("p (g c) -> p g c", g=RG), ALU.mult))
                    link(dve.tensor_reduce(slotf[:, :], slm[:, :, :], AX_X, ALU.add))
                    dve.tensor_scalar(of_batch(slot_all, b), slotf[:, :], 1.0, None, ALU.mult)
                    dve.tensor_scalar(of_batch(idx_rows[l], b), slotf[:, :], 1.0, None, ALU.mult)
                    dve.tensor_tensor(base[:, :], base[:, :], G_[:, RG * NPAIR:(RG + 1) * NPAIR],
                                      ALU.add).then_inc(slots_done, 1)

                def step(t, j, B):
                    if l == 0:
                        normalise(t, j)
                        maxima(t, j, 0)
                        normalise2(t, j)
                        first_moments(t, j, B)
                        leaky(t, j, 0)
                        weigh(t, j)
                        take_logits(t, j)
                        place(t, j, B)
                        residual(t, j)
                        choose(t, j, B)
                    else:
                        normalise(t, j)
                        maxima(t, j, 0)
                        normalise2(t, j)
                        maxima(t, j, 1)
                        leaky(t, j, 0)
                        first_moments(t, j, B)
                        maxima(t, j, 2)
                        leaky(t, j, 1)
                        weigh(t, j)
                        maxima(t, j, 3)
                        leaky(t, j, 2)
                        take_logits(t, j)
                        residual(t, j)
                        leaky(t, j, 3)
                        place(t, j, B)
                        choose(t, j, B)

                if l:
                    dve.wait_ge(padded, 16 * NPAIR)
                dve.tensor_copy(base[:, :], region).then_inc(base_reset, 1)
                dve.wait_ge(base_reset, l + 1)
                attention_steps(dve, step, RQ + 1)

                link = linker(plan, l * PLAN_LINKS, PLAN_LINKS)
                V = dve
                V.wait_ge(slots_done, (l + 1) * NB)
                link(V.tensor_copy(base_i[:, :], base[:, :]))
                link(V.tensor_tensor(cnt[:, :], base[:, :], region, ALU.subtract))
                link(V.tensor_scalar(cnt_i[:, :], cnt[:, :], float(P - 1), None, ALU.add))
                link(V.tensor_scalar(cnt_j[:, :], cnt_i[:, :], P.bit_length() - 1, None, ALU.arith_shift_right))
                link(V.tensor_copy(ntile[:, :], cnt_j[:, :]))
                link(V.tensor_tensor_scan(cum[:, :], ones_pair[:, :], ntile[:, :], 0.0, ALU.mult, ALU.add))
                link(V.tensor_tensor(shift[:, :], cum[:, :], ntile[:, :], ALU.subtract))
                link(V.scalar_tensor_tensor(shift[:, :], shift[:, :], float(P), region, ALU.mult, ALU.subtract))
                link(V.tensor_tensor(le[:, :, :], along(cum[:, :], 2), each(tile_no[:, :], NPAIR), ALU.is_le))
                for k, grow in enumerate((grow_region, grow_lower, grow_upper, ntile[:, :])):
                    link(V.tensor_tensor(lx[:, :, :], le[:, :, :], along(grow, 2), ALU.mult))
                    link(V.tensor_reduce(tvals[:, :, k] if k < 3 else tstart[:, :], lx[:, :, :], AX_X, ALU.add))
                link(V.tensor_scalar(tvals[:, :, 2], tvals[:, :, 2], 1.0, None, ALU.add))
                link(V.tensor_tensor(tvalid[:, :], cum[:, NPAIR - 1:NPAIR].to_broadcast([P, 2]), tile_no[:, :],
                                     ALU.is_gt))
                link(V.tensor_tensor(tstart[:, :], tile_no[:, :], tstart[:, :], ALU.subtract))
                link(V.tensor_tensor(tstart[:, :], tstart[:, :], tvalid[:, :], ALU.mult))
                V.scalar_tensor_tensor(tvals[:, :, 0], tstart[:, :], float(P), tvals[:, :, 0], ALU.mult,
                                       ALU.add).then_inc(tvals_done, 1)
                V.wait_ge(tableT_done, l + 1)
                V.tensor_copy(table[:, :], T2_[0:3, 0:TB]).then_inc(table_done, 1)

                link = linker(packed, l * PACK_LINKS, PACK_LINKS)
                V.wait_ge(b2_in, 16 * (l + 1))
                for k in range(3):
                    link(V.tensor_copy(b2_part[:, k, :], b2_rows[:, :]))
                    if k < 2:
                        link(V.tensor_tensor(b2_rows[:, :], b2_rows[:, :], b2_part[:, k, :], ALU.subtract))
                link(V.tensor_scalar(b2_rows[:, :], b2_part[:, 0, :], ident[0:3, 0:1], None, ALU.mult))
                link(V.scalar_tensor_tensor(b2_rows[:, :], b2_part[:, 1, :], ident[0:3, 1:2], b2_rows[:, :],
                                            ALU.mult, ALU.add))
                link(V.scalar_tensor_tensor(experts[0:3, :, 2 * HID + 2:PACK].bitcast(BF16),
                                            b2_part[:, 2, :].rearrange("p (e d) -> p e d", e=NE), ident[0:3, 2:3],
                                            b2_rows[:, :].rearrange("p (e d) -> p e d", e=NE), ALU.mult, ALU.add))
                V.wait_ge(experts_in, 16 * 3 * NE * (l + 1))
                V.wait_ge(table_done, l + 1)

                for b in range(NB):
                    link = linker(finding, (l * NB + b) * 3, 3)
                    link(V.tensor_tensor(slm[:, :, :], along(pairconst, RG), each(of_batch(code_all, b), NPAIR),
                                         ALU.is_equal))
                    link(V.tensor_tensor(slm[:, :, :], slm[:, :, :], along(shift[:, :], RG), ALU.mult))
                    link(V.tensor_reduce(slotf[:, :], slm[:, :, :], AX_X, ALU.add))
                    V.tensor_tensor(of_batch(gidx[l], b), of_batch(slot_all, b), slotf[:, :],
                                    ALU.add).then_inc(gidx_done, 1)

                def tile(t, j):
                    T = NT * l + t
                    if there(t, 0, NT):
                        col = slice(t, t + 1) if isinstance(t, int) else bass.ds(t, 1)
                        if l or since(t, 4):
                            held(y_done, T - 3)
                        for e in range(2):
                            expert = dve.value_load(table[1 + e:2 + e, col], min_val=0, max_val=NE - 1)
                            dve.tensor_copy(wst[j][:, e, :], experts[:, bass.ds(expert, 1), :].rearrange(
                                "p a c -> p (a c)")).then_inc(staged, 1)
                        dve.wait_ge(xs_in[j], (T - j) * 4 + 16)
                        if l or since(t, 2):
                            dve.wait_ge(xsT_done, T - 1)
                        dve.tensor_scalar(xsn[j % 2][:, :], xs[j][:, 0:P], xs[j][:, P:P + 1], xs[j][:, P + 1:P + 2],
                                          ALU.subtract, ALU.mult).then_inc(xsn_done, 1)
                    if there(t, 3, NT):
                        k = (j - 3) % 4
                        dve.wait_ge(y_done, T - 2)
                        dve.tensor_scalar(ya[k % 2][:, :], Y_[k % 2][:, 0:P], xs[k][:, P + 2:P + 3], None,
                                          ALU.mult).then_inc(ya_done, 1)
                        dve.wait_ge(ya_done, T - 2)
                        if l or since(t, 7):
                            dve.wait_ge(y_out[k], (T - 3 - k) * 4)
                        dve.scalar_tensor_tensor(yo[k][:, :], Y_[k % 2][:, P:2 * P], xs[k][:, P + 3:P + 4],
                                                 ya[k % 2][:, :], ALU.mult, ALU.add).then_inc(yo_done, 1)

                tile_steps(dve, tile, 3)

            def add_last(q, j, b):
                dve.wait_ge(gathered[j], (b + NB + 1) * (16 * QG))
                if since(q, 2):
                    dve.wait_ge(out_stored[j % 2], b * 32 + 16 * (j // 2))
                dve.tensor_tensor(osb[j % 2][:, :, :], xcols(q, 0, P), yg[j % 2][:, :, :],
                                  ALU.add).then_inc(out_added, 1)

            for j in range(RQ):
                add_last(j, j, 0)
            with dve.Fori(1, NB) as b:
                for j in range(RQ):
                    add_last(b * RQ + j, j, b)


def shape_constants(np, n_graphs):
    cap = n_graphs * P + P
    e = np.arange(NE)
    lo, hi = np.array(PAIRS).T
    region = np.arange(NPAIR) * cap
    grow = [np.diff(np.append(v, end)) for v, end in ((region, 0), (lo, 0), (hi, 1))]
    return np.concatenate([NE - e, 2.0 ** e, 2.0 ** (e + 1), 2.0 ** lo + 2.0 ** hi, region, *grow]).astype(np.float32)


_INS = ['x', 'adj', 'L0_gnn_W', 'L0_gnn_a', 'L0_ffn_Wg', 'L0_ffn_bg', 'L0_ffn_bias', 'L0_ffn_W1', 'L0_ffn_b1',
        'L0_ffn_W2', 'L0_ffn_b2', 'L1_gnn_W', 'L1_gnn_a', 'L1_ffn_gate_w', 'L1_ffn_gate_b', 'L1_ffn_W1',
        'L1_ffn_b1', 'L1_ffn_W2', 'L1_ffn_b2']


def build_from(nc, ap, out):
    build_program(nc, ap['x'], ap['adj'], (ap['L0_gnn_W'], ap['L1_gnn_W']), (ap['L0_gnn_a'], ap['L1_gnn_a']),
                  (ap['L0_ffn_Wg'], ap['L1_ffn_gate_w']), (ap['L0_ffn_bg'], ap['L0_ffn_bias'], ap['L1_ffn_gate_b']),
                  (ap['L0_ffn_W1'], ap['L1_ffn_W1']), (ap['L0_ffn_b1'], ap['L1_ffn_b1']),
                  (ap['L0_ffn_W2'], ap['L1_ffn_W2']), (ap['L0_ffn_b2'], ap['L1_ffn_b2']), ap['consts'], out)


def kernel(**inputs):
    import numpy as _np
    import concourse.bacc as _bacc
    from concourse import mybir as _mybir
    from concourse.bass_utils import run_bass_kernel_spmd as _run

    nc = _bacc.Bacc("TRN2", target_bir_lowering=False, num_devices=1)
    arrays, aps = {}, {}
    given = {name: _np.ascontiguousarray(inputs[name]) for name in _INS}
    given['consts'] = shape_constants(_np, given['x'].shape[0])
    for name, a in given.items():
        arrays[f"in_{name}_dram"] = a
        aps[name] = nc.dram_tensor(f"in_{name}_dram", a.shape, _mybir.dt.from_np(a.dtype), kind="ExternalInput").ap()
    out = nc.dram_tensor("out_dram", given['x'].shape, F32, kind="ExternalOutput").ap()
    build_from(nc, aps, out)
    r = _run(nc, [arrays], core_ids=[0])
    return r.results[0]["out_dram"]
```

```python
from contextlib import ExitStack

import concourse.bass as bass
from concourse import mybir

F32 = mybir.dt.float32
BF16 = mybir.dt.bfloat16
I32 = mybir.dt.int32
U32 = mybir.dt.uint32
ALU = mybir.AluOpType
ACT = mybir.ActivationFunctionType
AX_X = mybir.AxisListType.X

P = 128
QG = 4
TQ = 8
RQ = 4
NE = 8
HID = 256
PAIRS = [(a, b) for a in range(NE) for b in range(a + 1, NE)]
NPAIR = len(PAIRS)
ROW = P + 5
SECOND = HID + 2
LAST = SECOND + HID
PACK = LAST + P // 2
EPS = 1e-5
ALPHA = 0.2
MASKED = -9.0e15
NEVER = -3.0e38


def build_program(nc, x, adj, gnn_w, gnn_a, gate_w, gate_b, w1, b1, w2, b2, consts, out):
    NG = x.shape[0]
    NQ = NG // QG
    NB = NQ // RQ
    RG = QG * RQ
    NT = NG + NPAIR - 1
    CAP = NG * P + P
    HEADS = (1, gnn_w[1].shape[0])
    N_CONSTS = 7 + len(gate_b) + 2 * HEADS[1]
    ROUTE_LINKS, PLACE_LINKS, PLAN_LINKS, PACK_LINKS = 23, 3, 21, 8
    TB = 2 * P
    assert NT <= TB and NB >= 3 and P % HEADS[1] == 0

    rows_dram = nc.dram_tensor("rows_by_pair", (NPAIR * CAP + P, ROW), F32).ap()
    between = nc.dram_tensor("between_blocks", (NG, P, P), F32).ap()

    with ExitStack() as ctx:
        def sb(name, shape, dt=F32):
            return ctx.enter_context(nc.sbuf_tensor(name, shape, dt))

        def sem(name):
            return ctx.enter_context(nc.semaphore(name))

        X = sb("X", [P, NG, ROW])
        ident = sb("ident", [P, P])
        identb = sb("identb", [P, P], BF16)
        onesb = sb("onesb", [P, P], BF16)
        lower = sb("lower", [P, P], BF16)
        no_row = sb("no_row", [P, ROW])
        adj_i = sb("adj_i", [P, P], I32)
        maskneg = sb("maskneg", [P, P], BF16)
        W = [sb(f"W{l}", [P, P]) for l in range(2)]
        WT = [sb(f"WT{l}", [P, P]) for l in range(2)]
        A = [sb(f"A{l}", [P, 2, HEADS[l]]) for l in range(2)]
        wa1 = [sb(f"wa1_{l}", [P, HEADS[l], P]) for l in range(2)]
        wa2 = [sb(f"wa2_{l}", [P, HEADS[l], P]) for l in range(2)]
        Wg = [sb(f"Wg{l}", [P, NE]) for l in range(2)]
        gb_in = sb("gb_in", [P, 3, NE])
        gbias = [sb(f"gbias{l}", [P, NE]) for l in range(2)]
        experts = sb("experts", [P, NE, PACK])

        def two(name, shape, dt=F32):
            return [sb(f"{name}{k}", shape, dt) for k in range(2)]

        mv = two("mv", [P, QG, 2])
        mv2 = two("mv2", [P, QG, 2])
        st = two("st", [P, QG, 6])
        st2 = two("st2", [P, QG, 6])
        shift2 = two("shift2", [P, QG])
        neghalf = sb("neghalf", [P, QG])
        xn = two("xn", [P, QG, P])
        xnT = two("xnT", [P, QG * P])
        hsb = [sb(f"hsb{k}", [P, QG * P]) for k in range(4)]
        nmx = two("nmx", [P, 4])
        negm = [sb(f"negm{k}", [P, 4]) for k in range(4)]
        rel = two("rel", [P, 4 * P])
        es = two("es", [P, 4 * P])
        ps = two("ps", [P, 4 * P])
        pT = two("pT", [P, 4 * P])
        rowsum = [sb(f"rowsum{k}", [P, QG * max(HEADS)]) for k in range(4)]
        rinv = sb("rinv", [P, QG * max(HEADS)])
        hp = two("hp", [P, QG * P])
        mn = two("mn", [P, QG * P])
        ex = two("ex", [P, QG * P])
        xn2 = two("xn2", [P, QG, P])
        xn2T = two("xn2T", [P, QG * P])

        lg = sb("lg", [P, RG, NE])
        m1 = sb("m1", [P, RG])
        lm = sb("lm", [P, RG, NE])
        EX = sb("EX", [P, RG, NE])
        eq = sb("eq", [P, RG, NE])
        c1 = sb("c1", [P, RG])
        oh = sb("oh", [P, RG, NE])
        l2 = sb("l2", [P, RG, NE])
        sel = sb("sel", [P, RG, NE])
        tmp8 = sb("tmp8", [P, RG, NE])
        code = sb("code", [P, RG])
        den = sb("den", [P, RG])
        cw = sb("cw", [P, RG, NE])
        cwh = sb("cwh", [P, RG, NE])
        pc = sb("pc", [P, (RG + 1) * NPAIR], BF16)
        slm = sb("slm", [P, RG, NPAIR])
        slotf = sb("slotf", [P, RG])
        base = sb("base", [P, NPAIR])
        idx_rows = [sb(f"idx_rows{l}", [P, NG], U32) for l in range(2)]
        cst = sb("cst", [P, 3 * NE + 5 * NPAIR])
        revidx, pow2, pow2x2 = (cst[:, k * NE:(k + 1) * NE] for k in range(3))
        pairconst, region, grow_region, grow_lower, grow_upper = (
            cst[:, 3 * NE + k * NPAIR:3 * NE + (k + 1) * NPAIR] for k in range(5))
        ones_pair = sb("ones_pair", [P, NPAIR])
        tile_no = sb("tile_no", [P, 2])
        cnt = sb("cnt", [P, NPAIR])
        cnt_i = sb("cnt_i", [P, NPAIR], I32)
        cnt_j = sb("cnt_j", [P, NPAIR], I32)
        wpair = sb("wpair", [P, RG, 2])
        ntile = sb("ntile", [P, NPAIR])
        cum = sb("cum", [P, NPAIR])
        shift = sb("shift", [P, NPAIR])
        le = sb("le", [P, 2, NPAIR])
        lx = sb("lx", [P, 2, NPAIR])
        tvals = sb("tvals", [P, 2, 3])
        tstart = sb("tstart", [P, 2])
        tvalid = sb("tvalid", [P, 2])
        base_i = sb("base_i", [P, NPAIR], I32)
        table = sb("table", [3, TB], I32)

        xs = [sb(f"xs{k}", [P, ROW]) for k in range(TQ)]
        xsn = [sb(f"xsn{k}", [P, P]) for k in range(4)]
        xsT = two("xsT", [P, P])
        weights = sb("weights", [P, 4 * 2 * PACK])
        wst = [weights[:, k * 2 * PACK:(k + 1) * 2 * PACK].rearrange("p (e c) -> p e c", e=2) for k in range(4)]
        b2_rows = weights[0:3, 0:NE * P]
        b2_part = weights[0:3, NE * P:5 * NE * P // 2].bitcast(BF16).rearrange("p (k c) -> p k c", k=3)
        hh = two("hh", [P, 4, P])
        ya = two("ya", [P, P])
        yo = [sb(f"yo{k}", [P, P]) for k in range(4)]

        bank = [ctx.enter_context(nc.psum_tensor(f"bank{k}", [P, 512], F32)) for k in range(8)]
        T_, H_, E_, PT_, O_, G_ = bank[0], bank[1], bank[2:4], bank[4], bank[5:7], bank[7]
        XT_, HH_, Y_ = bank[0:2], bank[2:6], bank[6:8]

        consts_in, consts_dve, consts_pool = sem("consts_in"), sem("consts_dve"), sem("consts_pool")
        setup_pe, setup_act = sem("setup_pe"), sem("setup_act")
        experts_in, b2_in, packed = sem("experts_in"), sem("b2_in"), sem("packed")
        x_in = [sem(f"x_in{j}") for j in range(RQ)]
        moments, rstd, xn_ready = sem("moments"), sem("rstd"), sem("xn_ready")
        moments2, rstd2, xn2_ready = sem("moments2"), sem("rstd2"), sem("xn2_ready")
        stats_done, stats2_done, eps_added = sem("stats_done"), sem("stats2_done"), sem("eps_added")
        xT_done, xT_copied, h_done, h_copied = sem("xT_done"), sem("xT_copied"), sem("h_done"), sem("h_copied")
        s_done, max_done, negm_done = sem("s_done"), sem("max_done"), sem("negm_done")
        rel_done, e_done, p_done = sem("rel_done"), sem("e_done"), sem("p_done")
        pT_done, pT_copied, o_done = sem("pT_done"), sem("pT_copied"), sem("o_done")
        rinv_done, hp_done, mn_done, ex_done = sem("rinv_done"), sem("hp_done"), sem("mn_done"), sem("ex_done")
        pos_added, resid_done = sem("pos_added"), sem("resid_done")
        x2T_done, x2T_copied, logits_done, lg_done = sem("x2T_done"), sem("x2T_copied"), sem("logits_done"), sem("lg_done")
        route, lm_done, EX_done, pc_done = sem("route"), sem("lm_done"), sem("EX_done"), sem("pc_done")
        ranks_done, slots_done, scattered = sem("ranks_done"), sem("slots_done"), sem("scattered")
        plan, tvals_done, tableT_done, table_done = sem("plan"), sem("tvals_done"), sem("tableT_done"), sem("table_done")
        padded, absorbed = sem("padded"), sem("absorbed")
        staged_upper = sem("staged_upper")
        xs_in = [sem(f"xs_in{k}") for k in range(TQ)]
        xsn_done, staged, xsT_done, xsT_copied = sem("xsn_done"), sem("staged"), sem("xsT_done"), sem("xsT_copied")
        hh_done, act_done, y_done, ya_done, yo_done = sem("hh_done"), sem("act_done"), sem("y_done"), sem("ya_done"), sem("yo_done")
        y_out = [sem(f"y_out{k}") for k in range(4)]
        base_reset, placing = sem("base_reset"), sem("placing")
        centred, shifted, shift2_done = sem("centred"), sem("shifted"), sem("shift2_done")

        block = ctx.enter_context(nc.Block())

        def attention_steps(eng, step, tail):
            for t in range(2 * RQ):
                step(t, t % RQ, t // RQ)
            with eng.Fori(2, NB) as b:
                for j in range(RQ):
                    step(b * RQ + j, j, b)
            for t in range(NQ, NQ + tail):
                step(t, t % RQ, t // RQ)

        def tile_steps(eng, step, tail):
            for t in range(TQ):
                step(t, t % TQ, 0)
            with eng.Fori(1, NT // TQ) as b:
                for j in range(TQ):
                    step(b * TQ + j, j, b)
            for t in range(NT // TQ * TQ, NT + tail):
                step(t, t % TQ, t // TQ)

        def in_slot(k, n):
            return (NT - k + n - 1) // n

        def there(t, lag, n):
            return not isinstance(t, int) or 0 <= t - lag < n

        def wait(eng, s, value):
            if not isinstance(value, int) or value > 0:
                eng.wait_ge(s, value)

        UNITS = (1, QG)
        BEHIND = (dict(scores=-1, leaky=0, exps=0, turn=1, mix=1), dict(scores=-1, leaky=1, exps=1, turn=2, mix=3))

        def unit(l, t, j, u, stage):
            at = u - BEHIND[l][stage] if stage else u
            steps_back = 2 - at // UNITS[l]
            u = at % UNITS[l]
            q = t - steps_back
            return q, (j - steps_back) % 4, u, (q if l == 0 else NQ + q * QG + u), there(t, steps_back, NQ)

        def xcols(q, lo, hi):
            if isinstance(q, int):
                return X[:, QG * q:QG * q + QG, lo:hi]
            return X[:, bass.ds(q * QG, QG), lo:hi]

        def graph(q, g, lo, hi):
            if isinstance(q, int):
                return X[:, QG * q + g, lo:hi]
            return X[:, bass.ds(q * QG + g, 1), lo:hi].rearrange("p a d -> p (a d)")

        def of_batch(t, b):
            if isinstance(b, int):
                return t[:, RG * b:RG * b + RG]
            return t[:, bass.ds(b * RG, RG)]

        def each(t, n):
            return t.unsqueeze(2).to_broadcast([P, t.shape[1], n])

        def along(t, k):
            return t.unsqueeze(1).to_broadcast([P, k, t.shape[1]])

        def zero_ends(eng, pairs):
            for c in pairs:
                end = eng.value_load(base_i[0:1, c:c + 1], min_val=0, max_val=NPAIR * CAP - P)
                eng.dma_start(rows_dram[bass.ds(end, P), :], no_row[:, :]).then_inc(padded, 16)

        @block.sync
        def _(sp):
            loads = [(adj_i[:, :], adj), (W[0][:, :], gnn_w[0]),
                     (W[1][:, :].rearrange("p (h d) -> p h d", h=HEADS[1]), gnn_w[1].rearrange("h f d -> f h d")),
                     (Wg[0][:, :], gate_w[0]), (Wg[1][:, :], gate_w[1]),
                     (A[0][:, :, :].rearrange("p c h -> p (c h)"), gnn_a[0].rearrange("(c p) h -> p (c h)", c=2)),
                     (cst[:, :], consts.partition_broadcast(P))]
            for k, v in enumerate(gate_b):
                loads.append((gb_in[:, k, :], v.partition_broadcast(P)))
            for dst, src in loads:
                sp.dma_start(dst, src, allow_slow_non_contiguous=True).then_inc(consts_in, 16)
            sp.wait_ge(consts_pool, 1)
            hs = P // HEADS[1]
            for h in range(HEADS[1]):
                for c in range(2):
                    sp.dma_start(A[1][h * hs:(h + 1) * hs, c, h:h + 1],
                                 gnn_a[1][h:h + 1, c * hs:(c + 1) * hs].rearrange("a d -> d a"),
                                 allow_slow_non_contiguous=True).then_inc(consts_in, 16)

            def load_x(t, j, B):
                wait(sp, x_in[j], (B + l * NB) * 16)
                src = (between if l else x)
                src = src[QG * t:QG * t + QG] if isinstance(t, int) else src[bass.ds(t * QG, QG)]
                sp.dma_start(xcols(t, 0, P), src.rearrange("g p d -> p g d")).then_inc(x_in[j], 16)

            for l in range(2):
                attention_steps(sp, load_x, 0)

                if l == 0:
                    sp.wait_ge(consts_pool, 4)
                    sp.dma_start(rows_dram[NPAIR * CAP:NPAIR * CAP + P], no_row[:, :]).then_inc(padded, 16)
                else:
                    sp.wait_ge(staged, NT)
                    sp.wait_ge(staged_upper, NT)
                for e in range(NE):
                    sp.dma_start(experts[:, e, 0:HID], w1[l][e]).then_inc(experts_in, 16)
                    sp.dma_start(experts[:, e, SECOND:LAST].rearrange("p (c d) -> p c d", c=2),
                                 w2[l][e].rearrange("(c p) d -> p c d", c=2)).then_inc(experts_in, 16)
                    sp.dma_start(experts[:, e, HID:SECOND],
                                 b1[l][e].rearrange("(c p) -> p c", c=2),
                                 allow_slow_non_contiguous=True).then_inc(experts_in, 16)
                sp.dma_start(b2_rows[:, :], b2[l].rearrange("e d -> (e d)").partition_broadcast(3)).then_inc(b2_in, 16)

                sp.wait_ge(plan, (l + 1) * PLAN_LINKS)
                sp.wait_ge(scattered, 16 * NG * (l + 1))
                zero_ends(sp, range(0, NPAIR, 2))
                sp.wait_ge(padded, 16 * (NPAIR * (l + 1) + 1))
                sp.wait_ge(table_done, l + 1)

                def load_rows(t, j, b):
                    if there(t, 0, NT):
                        col = slice(t, t + 1) if isinstance(t, int) else bass.ds(t, 1)
                        row = sp.value_load(table[0:1, col], min_val=0, max_val=NPAIR * CAP)
                        if there(t, TQ, NT):
                            sp.wait_ge(y_out[j % 4], (b * 2 + (j // 4 - 1 + in_slot(j % 4, 4) * l)) * 16)
                        sp.dma_start(xs[j][:, :], rows_dram[bass.ds(row, P), :]).then_inc(xs_in[j], 16)

                tile_steps(sp, load_rows, 0)
                for k in range(4):
                    sp.wait_ge(y_out[k], 16 * in_slot(k, 4) * (l + 1))

        @block.gpsimd
        def _(pool):
            pool.memset(A[1][:, :, :], 0.0).then_inc(consts_pool, 1)
            pool.memset(experts[:, :, LAST:PACK], 0.0).then_inc(consts_pool, 1)
            pool.memset(onesb[:, :], 1.0)
            pool.memset(no_row[:, 0:ROW - 1], 0.0)
            pool.iota(no_row[:, ROW - 1:ROW].bitcast(I32), [[0, 1]], base=NG * P, channel_multiplier=1)
            pool.iota(X[:, :, ROW - 1:ROW].bitcast(I32).rearrange("p n a -> p (n a)"), [[P, NG]], base=0,
                      channel_multiplier=1)
            pool.memset(ones_pair[:, :], 1.0)
            pool.memset(neghalf[:, :], -0.5)
            pool.memset(pc[:, :], 0.0)
            pool.iota(tile_no[:, :], [[P, 2]], base=0, channel_multiplier=1, allow_small_or_imprecise_dtypes=True)
            pool.memset(lower[:, :], 0.0)
            pool.memset(identb[:, :], 0.0)
            pool.memset(ident[:, :], 0.0).then_inc(consts_pool, 1)
            pool.wait_ge(consts_pool, 3)
            pool.affine_select(out=ident[:, :], in_=ident[:, :], compare_op=ALU.not_equal, fill=1.0, base=0,
                               pattern=[[-1, P]], channel_multiplier=1)
            pool.affine_select(out=identb[:, :], in_=identb[:, :], compare_op=ALU.not_equal, fill=1.0, base=0,
                               pattern=[[-1, P]], channel_multiplier=1)
            pool.affine_select(out=lower[:, :], in_=lower[:, :], compare_op=ALU.is_ge, fill=1.0, base=0,
                               pattern=[[-1, P]], channel_multiplier=1).then_inc(consts_pool, 1)

            def pool_held(s, value):
                if not isinstance(value, int) or value > 0:
                    pool.wait_ge(s, value)
                    pool.sem_inc(absorbed, 1)

            n_eps = [0]

            def deviations(m, done, ready, n):
                pool.wait_ge(done, n)
                pool.tensor_scalar(m[:, :, 1], m[:, :, 1], EPS, None, ALU.add).then_inc(eps_added, 1)
                n_eps[0] += 1
                pool.wait_ge(eps_added, n_eps[0])
                pool.tensor_tensor(m[:, :, 1], m[:, :, 1], neghalf[:, :], ALU.pow).then_inc(ready, 1)
                pool.wait_ge(ready, n)

            def normalise(l, q):
                n = l * NQ + q + 1
                m = mv[q % 2]
                deviations(m, moments, rstd, n)
                wait(pool, xT_done, n - 2)
                pool.tensor_tensor(xn[q % 2][:, :, :], X[:, QG * q:QG * q + QG, 0:P], each(m[:, :, 0], P),
                                   ALU.subtract).then_inc(centred, 1)
                pool.wait_ge(centred, n)
                pool.tensor_tensor(xn[q % 2][:, :, :], xn[q % 2][:, :, :], each(m[:, :, 1], P),
                                   ALU.mult).then_inc(xn_ready, 1)

            def row_moments(l, q):
                n = l * NQ + q + 1
                m = mv2[q % 2]
                deviations(m, moments2, rstd2, n)
                pool.tensor_copy(X[:, QG * q:QG * q + QG, P:P + 2], m[:, :, :])
                pool.tensor_tensor(shift2[q % 2][:, :], m[:, :, 0], m[:, :, 1], ALU.mult).then_inc(shifted, 1)
                pool.wait_ge(shifted, n)
                pool.tensor_scalar(shift2[q % 2][:, :], shift2[q % 2][:, :], -1.0, None,
                                   ALU.mult).then_inc(shift2_done, 1)

            for l in range(2):
                for t in range(NQ + 4 * RQ):
                    if t < NQ:
                        normalise(l, t)
                    if 0 <= t - 4 < NQ:
                        row_moments(l, t - 4)
                    b, part = divmod(t - 12, RQ)
                    if 0 <= b < NB:
                        pool.wait_ge(slots_done, l * NB + b + 1)
                        for n in range(RG * b + QG * part, RG * b + QG * part + QG):
                            pool.indirect_dma_start(rows_dram,
                                                    bass.IndirectOffsetOnAxis(ap=idx_rows[l][:, n:n + 1], axis=0),
                                                    X[:, n, :], None).then_inc(scattered, 16)

                result = (out if l else between).rearrange("g p d -> (g p) d")

                def store_rows(t, j, b):
                    if there(t, 0, NT):
                        pool_held(yo_done, NT * l + t + 1)
                        pool.indirect_dma_start(result, bass.IndirectOffsetOnAxis(
                            ap=xs[j][:, ROW - 1:ROW].bitcast(U32), axis=0), yo[j % 4][:, :], None,
                            bounds_check=NG * P - 1, oob_is_err=False).then_inc(y_out[j % 4], 16)

                tile_steps(pool, store_rows, 0)

        @block.tensor
        def _(pe):
            pe.wait_ge(consts_pool, 4)
            pe.wait_ge(consts_in, 16 * N_CONSTS)
            for l in range(2):
                mm = pe.transpose(bank[l][:, 0:P], W[l][:, :], ident[:, :])
            mm.then_inc(setup_pe, 1)
            pe.wait_ge(setup_act, 2)
            for l in range(2):
                for c in range(2):
                    mm = pe.matmul(bank[2 + 2 * l + c][:, 0:HEADS[l] * P], WT[l][:, :], each(A[l][:, c, :], P),
                                   start=True, stop=True)
            mm.then_inc(setup_pe, 1)
            pe.wait_ge(setup_act, 6)
            pe.wait_ge(consts_dve, 3)

            for l in range(2):
                H = HEADS[l]
                hs = P // H

                def transposes(t, j):
                    if not there(t, 1, NQ):
                        return
                    if there(t, 5, NQ):
                        pe.wait_ge(x2T_copied, l * NQ + t - 4)
                    pe.wait_ge(xn_ready, l * NQ + t)
                    for g in range(QG):
                        mm = pe.transpose(T_[:, g * P:(g + 1) * P], xn[(j - 1) % 2][:, g, :], ident[:, :])
                    mm.then_inc(xT_done, 1)

                def project(t, j):
                    if not there(t, 1, NQ):
                        return
                    G = l * NQ + t - 1
                    wait(pe, h_copied, G)
                    pe.wait_ge(xT_copied, G + 1)
                    for g in range(QG):
                        mm = pe.matmul(H_[:, g * P:(g + 1) * P], xnT[(j - 1) % 2][:, g * P:(g + 1) * P], W[l][:, :],
                                       start=True, stop=True)
                    mm.then_inc(h_done, 1)

                def scores(t, j, u0):
                    q, ph, u, n, exists = unit(l, t, j, u0, "scores")
                    if not exists:
                        return
                    e = E_[ph % 2 if l == 0 else u % 2]
                    xT = xnT[ph % 2]
                    wait(pe, e_done, n - 1)
                    pe.matmul(e[:, :], identb[:, :], along(maskneg[:, :], 4), start=True, stop=False)
                    if l == 0:
                        pe.matmul(e[:, :], wa2[0][:, 0, :], xT[:, :], start=False, stop=False)
                        for g in range(QG):
                            mm = pe.matmul(e[:, g * P:(g + 1) * P], xT[:, g * P:(g + 1) * P], wa1[0][:, 0, :],
                                           start=False, stop=(g == QG - 1))
                    else:
                        xg = xT[:, u * P:(u + 1) * P]
                        pe.matmul(e[:, :], xg, wa1[1][:, :, :], start=False, stop=False)
                        for h in range(H):
                            mm = pe.matmul(e[:, h * P:(h + 1) * P], wa2[1][:, h, :], xg,
                                           start=False, stop=(h == H - 1))
                    mm.then_inc(s_done, 1)

                def turn(t, j, u0):
                    q, ph, u, n, exists = unit(l, t, j, u0, "turn")
                    if not exists:
                        return
                    k = ph % 2 if l == 0 else u % 2
                    pe.wait_ge(p_done, n + 1)
                    for i in range(4):
                        mm = pe.transpose(PT_[:, i * P:(i + 1) * P], ps[k][:, i * P:(i + 1) * P], ident[:, :])
                    mm.then_inc(pT_done, 1)

                def mix(t, j, u0):
                    q, ph, u, n, exists = unit(l, t, j, u0, "mix")
                    if not exists:
                        return
                    G = l * NQ + q
                    k = ph % 2 if l == 0 else u % 2
                    if u == 0:
                        pe.wait_ge(h_copied, G + 1)
                        wait(pe, hp_done, G - 1)
                    pe.wait_ge(pT_copied, n + 1)
                    for i in range(4):
                        p_i = pT[k][:, i * P:(i + 1) * P]
                        if l == 0:
                            c = slice(i * P, (i + 1) * P)
                        else:
                            c = slice(u * P + i * hs, u * P + (i + 1) * hs)
                        mm = pe.matmul(O_[ph % 2][:, c], p_i, hsb[ph][:, c], start=True, stop=True)
                    mm.then_inc(o_done, 1)

                def transposes2(t, j):
                    if not there(t, 5, NQ):
                        return
                    pe.wait_ge(xn2_ready, l * NQ + t - 4)
                    for g in range(QG):
                        mm = pe.transpose(T_[:, g * P:(g + 1) * P], xn2[(j - 5) % 2][:, g, :], ident[:, :])
                    mm.then_inc(x2T_done, 1)

                def logits(t, j, B):
                    if not there(t, 5, NQ):
                        return
                    G = l * NQ + t - 5
                    wait(pe, lg_done, G)
                    if j == 3 and not (isinstance(t, int) and B < 2):
                        pe.wait_ge(slots_done, l * NB + B - 1)
                    pe.wait_ge(x2T_copied, G + 1)
                    for g in range(QG):
                        mm = pe.matmul(G_[:, 480 + g * NE:480 + (g + 1) * NE],
                                       xn2T[(j - 5) % 2][:, g * P:(g + 1) * P], Wg[l][:, :], start=True, stop=True)
                    mm.then_inc(logits_done, 1)

                def ranks(t, j, B):
                    if j != 2 or not there(t, 10, NQ):
                        return
                    width = (RG + 1) * NPAIR
                    pe.wait_ge(pc_done, l * NB + B - 1)
                    pe.wait_ge(lg_done, l * NQ + (min(t - 5, NQ) if isinstance(t, int) else t - 5))
                    pe.matmul(G_[:, 0:width], lower[:, :], pc[:, :], start=True, stop=False)
                    for s in range(1, RG + 1):
                        mm = pe.matmul(G_[:, s * NPAIR:width], onesb[:, :], pc[:, 0:width - s * NPAIR],
                                       start=False, stop=(s == RG))
                    mm.then_inc(ranks_done, 1)

                def step(t, j, B):
                    if l == 0:
                        turn(t, j, 0)
                        transposes2(t, j)
                        mix(t, j, 0)
                        transposes(t, j)
                        logits(t, j, B)
                        project(t, j)
                        scores(t, j, 0)
                        ranks(t, j, B)
                    else:
                        for u in range(4):
                            mix(t, j, u)
                            turn(t, j, u)
                            scores(t, j, u)
                            if u == 0:
                                transposes2(t, j)
                            elif u == 1:
                                transposes(t, j)
                                logits(t, j, B)
                            elif u == 2:
                                project(t, j)
                                ranks(t, j, B)

                attention_steps(pe, step, 11)

                pe.wait_ge(tvals_done, l + 1)
                for c in range(2):
                    mm = pe.transpose(T_[0:3, c * P:(c + 1) * P], tvals[:, c, :], ident[:, :])
                mm.then_inc(tableT_done, 1)

                def tile(t, j, b):
                    T = NT * l + t
                    if there(t, 0, NT):
                        pe.wait_ge(xsn_done, T + 1)
                        pe.transpose(XT_[j % 2][:, 0:P], xsn[j % 4][:, :], ident[:, :]).then_inc(xsT_done, 1)
                    if there(t, 1, NT):
                        k = (j - 1) % 4
                        pe.wait_ge(staged, T)
                        pe.wait_ge(staged_upper, T)
                        pe.wait_ge(xsT_copied, T)
                        for c in range(4):
                            mm = pe.matmul(HH_[k][:, c * P:(c + 1) * P],
                                           wst[k][:, c // 2, (c % 2) * P:(c % 2 + 1) * P], xsT[k % 2][:, :],
                                           start=True, stop=True)
                        mm.then_inc(hh_done, 1)
                    if there(t, 2, NT):
                        k = (j - 2) % 4
                        wait(pe, yo_done, T - 3)
                        pe.wait_ge(act_done, T - 1)
                        for e in range(2):
                            y = Y_[k % 2][:, e * P:(e + 1) * P]
                            pe.matmul(y, onesb[0:3, :], wst[k][0:3, e, LAST:PACK].bitcast(BF16),
                                      start=True, stop=False)
                            for c in range(2):
                                mm = pe.matmul(y, hh[k % 2][:, 2 * e + c, :],
                                               wst[k][:, e, SECOND + c * P:SECOND + (c + 1) * P],
                                               start=False, stop=(c == 1))
                        mm.then_inc(y_done, 1)

                tile_steps(pe, tile, 2)

        @block.scalar
        def _(act):
            act.preload_act_table_set("exp_and_others")
            act.wait_ge(setup_pe, 1)
            for l in range(2):
                act.activation(WT[l][:, :], bank[l][:, 0:P], ACT.Copy).then_inc(setup_act, 1)
            act.wait_ge(setup_pe, 2)
            for l in range(2):
                for c, wa in enumerate((wa1, wa2)):
                    act.activation(wa[l][:, :, :].rearrange("p h d -> p (h d)"),
                                   bank[2 + 2 * l + c][:, 0:HEADS[l] * P], ACT.Copy).then_inc(setup_act, 1)

            for l in range(2):
                H = HEADS[l]

                def copy_xT(t, j):
                    if there(t, 1, NQ):
                        act.wait_ge(xT_done, l * NQ + t)
                        act.activation(xnT[(j - 1) % 2][:, :], T_[:, :], ACT.Copy).then_inc(xT_copied, 1)

                def copy_h(t, j):
                    if there(t, 1, NQ):
                        act.wait_ge(h_done, l * NQ + t)
                        act.activation(hsb[(j - 1) % 4][:, :], H_[:, :], ACT.Copy).then_inc(h_copied, 1)

                def rectify(t, j, u0):
                    q, ph, u, n, exists = unit(l, t, j, u0, None)
                    if exists:
                        k = ph % 2 if l == 0 else u % 2
                        act.wait_ge(max_done, n + 1)
                        act.activation(rel[k][:, :], E_[k][:, :], ACT.Relu, scale=1.0 - ALPHA).then_inc(rel_done, 1)

                def exps(t, j, u0):
                    q, ph, u, n, exists = unit(l, t, j, u0, "exps")
                    if exists:
                        k = ph % 2 if l == 0 else u % 2
                        act.wait_ge(e_done, n + 1)
                        for i in range(4):
                            ins = act.activation(ps[k][:, i * P:(i + 1) * P], es[k][:, i * P:(i + 1) * P], ACT.Exp,
                                                 bias=negm[ph if l == 0 else u][:, i:i + 1],
                                                 accum_out=rowsum[ph][:, 4 * u + i:4 * u + i + 1])
                        ins.then_inc(p_done, 1)

                def copy_pT(t, j, u0):
                    q, ph, u, n, exists = unit(l, t, j, u0, "turn")
                    if exists:
                        k = ph % 2 if l == 0 else u % 2
                        act.wait_ge(pT_done, n + 1)
                        act.activation(pT[k][:, :], PT_[:, :], ACT.Copy).then_inc(pT_copied, 1)

                def exp_neg(t, j):
                    if there(t, 4, NQ):
                        act.wait_ge(mn_done, l * NQ + t - 3)
                        act.activation(ex[j % 2][:, :], mn[j % 2][:, :], ACT.Exp).then_inc(ex_done, 1)

                def normalise2(t, j):
                    if there(t, 5, NQ):
                        k = (j - 5) % 2
                        act.wait_ge(shift2_done, l * NQ + t - 4)
                        for g in range(QG):
                            ins = act.activation(xn2[k][:, g, :], graph(t - 5, g, 0, P), ACT.Identity,
                                                 bias=shift2[k][:, g:g + 1], scale=mv2[k][:, g, 1:2])
                        ins.then_inc(xn2_ready, 1)

                def copy_x2T(t, j):
                    if there(t, 5, NQ):
                        act.wait_ge(x2T_done, l * NQ + t - 4)
                        act.activation(xn2T[(j - 5) % 2][:, :], T_[:, :], ACT.Copy).then_inc(x2T_copied, 1)

                def exp_logits(t, j, B):
                    if j == 1 and there(t, 9, NQ):
                        act.wait_ge(lm_done, l * NB + B - 1)
                        act.activation(EX[:, :, :], lm[:, :, :], ACT.Exp).then_inc(EX_done, 1)

                def step(t, j, B):
                    if l == 0:
                        normalise2(t, j)
                        copy_pT(t, j, 0)
                        copy_x2T(t, j)
                        copy_xT(t, j)
                        rectify(t, j, 0)
                        exp_neg(t, j)
                        copy_h(t, j)
                        exps(t, j, 0)
                        exp_logits(t, j, B)
                    else:
                        normalise2(t, j)
                        for u in range(4):
                            rectify(t, j, u)
                            exps(t, j, u)
                            copy_pT(t, j, u)
                            if u == 0:
                                copy_x2T(t, j)
                            elif u == 1:
                                copy_xT(t, j)
                            elif u == 2:
                                exp_neg(t, j)
                            else:
                                copy_h(t, j)
                                exp_logits(t, j, B)

                attention_steps(act, step, 10)
                if l:
                    act.preload_act_table_set("gelu_and_others")
                act.wait_ge(plan, (l + 1) * PLAN_LINKS)
                act.wait_ge(scattered, 16 * NG * (l + 1))
                zero_ends(act, range(1, NPAIR, 2))
                func = ACT.Gelu if l else ACT.Relu
                act.wait_ge(experts_in, 16 * 3 * NE * (l + 1))
                act.wait_ge(packed, (l + 1) * PACK_LINKS)
                act.wait_ge(table_done, l + 1)

                def tile(t, j, b):
                    T = NT * l + t
                    if there(t, 0, NT):
                        col = slice(t, t + 1) if isinstance(t, int) else bass.ds(t, 1)
                        expert = act.value_load(table[2:3, col], min_val=0, max_val=NE - 1)
                        act.activation(wst[j % 4][:, 1, :], experts[:, bass.ds(expert, 1), :].rearrange(
                            "p a c -> p (a c)"), ACT.Copy).then_inc(staged_upper, 1)
                        act.wait_ge(xsT_done, T + 1)
                        act.activation(xsT[j % 2][:, :], XT_[j % 2][:, 0:P], ACT.Copy).then_inc(xsT_copied, 1)
                    if there(t, 1, NT):
                        k = (j - 1) % 4
                        act.wait_ge(hh_done, T)
                        for c in range(4):
                            ins = act.activation(hh[k % 2][:, c, :], HH_[k][:, c * P:(c + 1) * P], func,
                                                 bias=wst[k][:, c // 2, HID + c % 2:HID + c % 2 + 1])
                        ins.then_inc(act_done, 1)

                tile_steps(act, tile, 1)
                if l == 0:
                    act.preload_act_table_set("exp_and_others")

        @block.vector
        def _(dve):
            def linker(s, before, links):
                done = [0]

                def run(ins):
                    done[0] += 1
                    assert done[0] <= links
                    ins.then_inc(s, 1)
                    dve.wait_ge(s, before + done[0])
                return run

            def held(s, value):
                dve.wait_ge(s, value)
                dve.sem_inc(absorbed, 1)

            dve.wait_ge(consts_in, 16 * N_CONSTS)
            dve.tensor_scalar(maskneg[:, :], adj_i[:, :], 0, MASKED, ALU.is_le, ALU.mult).then_inc(consts_dve, 1)
            dve.tensor_tensor(gbias[0][:, :], gb_in[:, 0, :], gb_in[:, 1, :], ALU.add).then_inc(consts_dve, 1)
            dve.tensor_copy(gbias[1][:, :], gb_in[:, 2, :]).then_inc(consts_dve, 1)
            dve.wait_ge(consts_pool, 4)

            for l in range(2):
                H = HEADS[l]

                def first_moments(t, j, B):
                    if not there(t, 0, NQ):
                        return
                    held(x_in[j], (B + (l * NB + 1)) * 16)
                    for g in range(QG):
                        dve.bn_stats(st[j % 2][:, g, :], graph(t, g, 0, P)).then_inc(stats_done, 1)
                    held(stats_done, (l * NQ + t + 1) * QG)
                    for g in range(QG):
                        ins = dve.bn_aggr(mv[j % 2][:, g, :], st[j % 2][:, g, :])
                    ins.then_inc(moments, 1)

                def maxima(t, j, u0):
                    q, ph, u, n, exists = unit(l, t, j, u0, None)
                    if not exists:
                        return
                    k = ph % 2 if l == 0 else u % 2
                    dve.wait_ge(s_done, n + 1)
                    dve.tensor_reduce(nmx[k][:, :], E_[k][:, :].rearrange("p (b c) -> p b c", b=4), AX_X, ALU.max,
                                      negate=True).then_inc(max_done, 1)
                    dve.wait_ge(max_done, n + 1)
                    dve.scalar_tensor_tensor(negm[ph if l == 0 else u][:, :], nmx[k][:, :], ALPHA, nmx[k][:, :],
                                             ALU.mult, ALU.min)

                def leaky(t, j, u0):
                    q, ph, u, n, exists = unit(l, t, j, u0, "leaky")
                    if not exists:
                        return
                    k = ph % 2 if l == 0 else u % 2
                    dve.wait_ge(rel_done, n + 1)
                    dve.scalar_tensor_tensor(es[k][:, :], E_[k][:, :], ALPHA, rel[k][:, :], ALU.mult,
                                             ALU.add).then_inc(e_done, 1)

                def weigh(t, j):
                    if not there(t, 4, NQ):
                        return
                    G = l * NQ + t - 4
                    k = j % 2
                    dve.wait_ge(o_done, t - 3 if l == 0 else NQ + (t - 3) * QG)
                    dve.reciprocal(rinv[:, 0:QG * H], rowsum[j][:, 0:QG * H]).then_inc(rinv_done, 1)
                    dve.wait_ge(rinv_done, G + 1)
                    dve.tensor_tensor(hp[k][:, :].rearrange("p (b c) -> p b c", b=QG * H),
                                      O_[j % 2][:, :].rearrange("p (b c) -> p b c", b=QG * H),
                                      each(rinv[:, 0:QG * H], P // H), ALU.mult).then_inc(hp_done, 1)
                    dve.wait_ge(hp_done, G + 1)
                    dve.tensor_scalar(mn[k][:, :], hp[k][:, :], 0.0, None, ALU.min).then_inc(mn_done, 1)

                def residual(t, j):
                    if not there(t, 4, NQ):
                        return
                    q = t - 4
                    G = l * NQ + q
                    k = j % 2
                    h3 = hp[k][:, :].rearrange("p (g d) -> p g d", g=QG)
                    dve.scalar_tensor_tensor(h3, h3, 0.0, xcols(q, 0, P), ALU.max, ALU.add).then_inc(pos_added, 1)
                    dve.wait_ge(pos_added, G + 1)
                    dve.wait_ge(ex_done, G + 1)
                    dve.scalar_tensor_tensor(xcols(q, 0, P), ex[k][:, :].rearrange("p (g d) -> p g d", g=QG), -1.0,
                                             h3, ALU.add, ALU.add).then_inc(resid_done, 1)
                    held(resid_done, G + 1)
                    for g in range(QG):
                        dve.bn_stats(st2[k][:, g, :], graph(q, g, 0, P)).then_inc(stats2_done, 1)
                    held(stats2_done, (G + 1) * QG)
                    for g in range(QG):
                        ins = dve.bn_aggr(mv2[k][:, g, :], st2[k][:, g, :])
                    ins.then_inc(moments2, 1)

                def take_logits(t, j):
                    if not there(t, 6, NQ):
                        return
                    ph = (j - 6) % 4
                    dve.wait_ge(logits_done, l * NQ + t - 5)
                    dve.tensor_tensor(lg[:, QG * ph:QG * ph + QG, :],
                                      G_[:, 480:480 + QG * NE].rearrange("p (g e) -> p g e", g=QG),
                                      along(gbias[l][:, :], QG), ALU.add).then_inc(lg_done, 1)

                def choose(t, j, B):
                    if j != 1 or not there(t, 9, NQ):
                        return
                    b = B - 2
                    N = l * NB + b
                    link = linker(route, N * ROUTE_LINKS, ROUTE_LINKS)
                    V = dve
                    V.wait_ge(lg_done, (N + 1) * RQ)
                    link(V.tensor_reduce(m1[:, :], lg[:, :, :], AX_X, ALU.max))
                    V.tensor_tensor(lm[:, :, :], lg[:, :, :], each(m1[:, :], NE), ALU.subtract).then_inc(lm_done, 1)

                    def first_of(values, peak, onehot):
                        link(V.tensor_tensor(eq[:, :, :], values, each(peak, NE), ALU.is_equal))
                        link(V.tensor_tensor(eq[:, :, :], eq[:, :, :], along(revidx, RG), ALU.mult))
                        link(V.tensor_reduce(c1[:, :], eq[:, :, :], AX_X, ALU.max))
                        link(V.tensor_tensor(onehot, eq[:, :, :], each(c1[:, :], NE), ALU.is_equal))

                    first_of(lg[:, :, :], m1[:, :], oh[:, :, :])
                    link(V.scalar_tensor_tensor(l2[:, :, :], oh[:, :, :], NEVER, lg[:, :, :], ALU.mult, ALU.add))
                    link(V.tensor_reduce(m1[:, :], l2[:, :, :], AX_X, ALU.max))
                    first_of(l2[:, :, :], m1[:, :], sel[:, :, :])
                    link(V.tensor_tensor(sel[:, :, :], sel[:, :, :], oh[:, :, :], ALU.add))
                    link(V.tensor_tensor(tmp8[:, :, :], sel[:, :, :], along(pow2, RG), ALU.mult))
                    link(V.tensor_reduce(code[:, :], tmp8[:, :, :], AX_X, ALU.add))
                    V.tensor_tensor(pc[:, 0:RG * NPAIR].rearrange("p (g c) -> p g c", g=RG), along(pairconst, RG),
                                    each(code[:, :], NPAIR), ALU.is_equal).then_inc(pc_done, 1)
                    V.wait_ge(EX_done, N + 1)
                    link(V.tensor_tensor(tmp8[:, :, :], sel[:, :, :], EX[:, :, :], ALU.mult))
                    link(V.tensor_reduce(den[:, :], (EX if l else tmp8)[:, :, :], AX_X, ALU.add))
                    link(V.reciprocal(den[:, :], den[:, :]))
                    link(V.tensor_tensor(cw[:, :, :], tmp8[:, :, :], each(den[:, :], NE), ALU.mult))
                    link(V.tensor_tensor(cwh[:, :, :], along(pow2x2, RG), each(code[:, :], NE), ALU.is_gt))
                    link(V.tensor_tensor(cwh[:, :, :], cwh[:, :, :], cw[:, :, :], ALU.mult))
                    link(V.tensor_reduce(wpair[:, :, 1], cwh[:, :, :], AX_X, ALU.add))
                    link(V.tensor_tensor(cw[:, :, :], cw[:, :, :], cwh[:, :, :], ALU.subtract))
                    link(V.tensor_reduce(wpair[:, :, 0], cw[:, :, :], AX_X, ALU.add))
                    V.tensor_scalar(xcols_of_batch(b, P + 2, P + 4), wpair[:, :, :], 1.0, None, ALU.mult)

                def xcols_of_batch(b, lo, hi):
                    if isinstance(b, int):
                        return X[:, RG * b:RG * b + RG, lo:hi]
                    return X[:, bass.ds(b * RG, RG), lo:hi]

                def place(t, j, B):
                    if j != 3 or not there(t, 11, NQ):
                        return
                    b = B - 2
                    N = l * NB + b
                    link = linker(placing, N * PLACE_LINKS, PLACE_LINKS)
                    dve.wait_ge(ranks_done, N + 1)
                    ranks = G_[:, 0:RG * NPAIR].rearrange("p (g c) -> p g c", g=RG)
                    link(dve.tensor_tensor(slm[:, :, :], ranks, along(base[:, :], RG), ALU.add))
                    link(dve.tensor_tensor(slm[:, :, :], slm[:, :, :],
                                           pc[:, 0:RG * NPAIR].rearrange("p (g c) -> p g c", g=RG), ALU.mult))
                    link(dve.tensor_reduce(slotf[:, :], slm[:, :, :], AX_X, ALU.add))
                    dve.tensor_scalar(of_batch(idx_rows[l], b), slotf[:, :], 1.0, None, ALU.mult)
                    dve.tensor_tensor(base[:, :], base[:, :], G_[:, RG * NPAIR:(RG + 1) * NPAIR],
                                      ALU.add).then_inc(slots_done, 1)

                def step(t, j, B):
                    if l == 0:
                        maxima(t, j, 0)
                        weigh(t, j)
                        place(t, j, B)
                        take_logits(t, j)
                        leaky(t, j, 0)
                        first_moments(t, j, B)
                        residual(t, j)
                        choose(t, j, B)
                    else:
                        for u in range(4):
                            leaky(t, j, u)
                            maxima(t, j, u)
                            if u == 0:
                                place(t, j, B)
                                take_logits(t, j)
                            elif u == 1:
                                first_moments(t, j, B)
                                weigh(t, j)
                            elif u == 2:
                                residual(t, j)
                            else:
                                choose(t, j, B)

                link = linker(packed, l * PACK_LINKS, PACK_LINKS)
                dve.wait_ge(b2_in, 16 * (l + 1))
                for k in range(3):
                    link(dve.tensor_copy(b2_part[:, k, :], b2_rows[:, :]))
                    if k < 2:
                        link(dve.tensor_tensor(b2_rows[:, :], b2_rows[:, :], b2_part[:, k, :], ALU.subtract))
                link(dve.tensor_scalar(b2_rows[:, :], b2_part[:, 0, :], ident[0:3, 0:1], None, ALU.mult))
                link(dve.scalar_tensor_tensor(b2_rows[:, :], b2_part[:, 1, :], ident[0:3, 1:2], b2_rows[:, :],
                                            ALU.mult, ALU.add))
                link(dve.scalar_tensor_tensor(experts[0:3, :, LAST:PACK].bitcast(BF16),
                                            b2_part[:, 2, :].rearrange("p (e d) -> p e d", e=NE), ident[0:3, 2:3],
                                            b2_rows[:, :].rearrange("p (e d) -> p e d", e=NE), ALU.mult, ALU.add))
                if l:
                    dve.wait_ge(padded, 16 * (NPAIR + 1))
                dve.tensor_copy(base[:, :], region).then_inc(base_reset, 1)
                dve.wait_ge(base_reset, l + 1)
                attention_steps(dve, step, 12)

                link = linker(plan, l * PLAN_LINKS, PLAN_LINKS)
                V = dve
                V.wait_ge(slots_done, (l + 1) * NB)
                link(V.tensor_copy(base_i[:, :], base[:, :]))
                link(V.tensor_tensor(cnt[:, :], base[:, :], region, ALU.subtract))
                link(V.tensor_scalar(cnt_i[:, :], cnt[:, :], float(P - 1), None, ALU.add))
                link(V.tensor_scalar(cnt_j[:, :], cnt_i[:, :], P.bit_length() - 1, None, ALU.arith_shift_right))
                link(V.tensor_copy(ntile[:, :], cnt_j[:, :]))
                link(V.tensor_tensor_scan(cum[:, :], ones_pair[:, :], ntile[:, :], 0.0, ALU.mult, ALU.add))
                link(V.tensor_tensor(shift[:, :], cum[:, :], ntile[:, :], ALU.subtract))
                link(V.scalar_tensor_tensor(shift[:, :], shift[:, :], float(P), region, ALU.mult, ALU.subtract))
                link(V.tensor_tensor(le[:, :, :], along(cum[:, :], 2), each(tile_no[:, :], NPAIR), ALU.is_le))
                for k, grow in enumerate((grow_region, grow_lower, grow_upper, ntile[:, :])):
                    link(V.tensor_tensor(lx[:, :, :], le[:, :, :], along(grow, 2), ALU.mult))
                    link(V.tensor_reduce(tvals[:, :, k] if k < 3 else tstart[:, :], lx[:, :, :], AX_X, ALU.add))
                link(V.tensor_scalar(tvals[:, :, 2], tvals[:, :, 2], 1.0, None, ALU.add))
                link(V.tensor_tensor(tvalid[:, :], cum[:, NPAIR - 1:NPAIR].to_broadcast([P, 2]), tile_no[:, :],
                                     ALU.is_gt))
                link(V.tensor_tensor(tstart[:, :], tile_no[:, :], tstart[:, :], ALU.subtract))
                link(V.tensor_tensor(tstart[:, :], tstart[:, :], tvalid[:, :], ALU.mult))
                V.scalar_tensor_tensor(tvals[:, :, 0], tstart[:, :], float(P), tvals[:, :, 0], ALU.mult,
                                       ALU.add).then_inc(tvals_done, 1)
                V.wait_ge(tableT_done, l + 1)
                V.tensor_copy(table[:, :], T_[0:3, 0:TB]).then_inc(table_done, 1)

                V.wait_ge(experts_in, 16 * 3 * NE * (l + 1))
                V.wait_ge(table_done, l + 1)

                def tile(t, j, b):
                    T = NT * l + t
                    if there(t, 0, NT):
                        col = slice(t, t + 1) if isinstance(t, int) else bass.ds(t, 1)
                        held(xs_in[j], (b + (in_slot(j, TQ) * l + 1)) * 16)
                        expert = dve.value_load(table[1:2, col], min_val=0, max_val=NE - 1)
                        dve.tensor_scalar(xsn[j % 4][:, :], xs[j][:, 0:P], xs[j][:, P:P + 1], xs[j][:, P + 1:P + 2],
                                          ALU.subtract, ALU.mult).then_inc(xsn_done, 1)
                        dve.tensor_copy(wst[j % 4][:, 0, :], experts[:, bass.ds(expert, 1), :].rearrange(
                            "p a c -> p (a c)")).then_inc(staged, 1)
                    if there(t, 3, NT):
                        k = (j - 3) % 4
                        row = xs[(j - 3) % TQ]
                        wait(dve, y_out[k], (b * 2 + ((j - 3) // 4 + in_slot(k, 4) * l)) * 16)
                        dve.wait_ge(y_done, T - 2)
                        dve.scalar_tensor_tensor(ya[k % 2][:, :], Y_[k % 2][:, 0:P], row[:, P + 2:P + 3],
                                                 row[:, 0:P], ALU.mult, ALU.add).then_inc(ya_done, 1)
                        dve.wait_ge(ya_done, T - 2)
                        dve.scalar_tensor_tensor(yo[k][:, :], Y_[k % 2][:, P:2 * P], row[:, P + 3:P + 4],
                                                 ya[k % 2][:, :], ALU.mult, ALU.add).then_inc(yo_done, 1)

                tile_steps(dve, tile, 3)


def shape_constants(np, n_graphs):
    cap = n_graphs * P + P
    e = np.arange(NE)
    lo, hi = np.array(PAIRS).T
    region = np.arange(NPAIR) * cap
    grow = [np.diff(np.append(v, end)) for v, end in ((region, NPAIR * cap), (lo, 0), (hi, 1))]
    return np.concatenate([NE - e, 2.0 ** e, 2.0 ** (e + 1), 2.0 ** lo + 2.0 ** hi, region, *grow]).astype(np.float32)


_INS = ['x', 'adj', 'L0_gnn_W', 'L0_gnn_a', 'L0_ffn_Wg', 'L0_ffn_bg', 'L0_ffn_bias', 'L0_ffn_W1', 'L0_ffn_b1',
        'L0_ffn_W2', 'L0_ffn_b2', 'L1_gnn_W', 'L1_gnn_a', 'L1_ffn_gate_w', 'L1_ffn_gate_b', 'L1_ffn_W1',
        'L1_ffn_b1', 'L1_ffn_W2', 'L1_ffn_b2']


def build_from(nc, ap, out):
    build_program(nc, ap['x'], ap['adj'], (ap['L0_gnn_W'], ap['L1_gnn_W']), (ap['L0_gnn_a'], ap['L1_gnn_a']),
                  (ap['L0_ffn_Wg'], ap['L1_ffn_gate_w']), (ap['L0_ffn_bg'], ap['L0_ffn_bias'], ap['L1_ffn_gate_b']),
                  (ap['L0_ffn_W1'], ap['L1_ffn_W1']), (ap['L0_ffn_b1'], ap['L1_ffn_b1']),
                  (ap['L0_ffn_W2'], ap['L1_ffn_W2']), (ap['L0_ffn_b2'], ap['L1_ffn_b2']), ap['consts'], out)


def kernel(**inputs):
    import numpy as _np
    import concourse.bacc as _bacc
    from concourse import mybir as _mybir
    from concourse.bass_utils import run_bass_kernel_spmd as _run

    nc = _bacc.Bacc("TRN2", target_bir_lowering=False, num_devices=1)
    arrays, aps = {}, {}
    given = {name: _np.ascontiguousarray(inputs[name]) for name in _INS}
    given['consts'] = shape_constants(_np, given['x'].shape[0])
    for name, a in given.items():
        arrays[f"in_{name}_dram"] = a
        aps[name] = nc.dram_tensor(f"in_{name}_dram", a.shape, _mybir.dt.from_np(a.dtype), kind="ExternalInput").ap()
    out = nc.dram_tensor("out_dram", given['x'].shape, F32, kind="ExternalOutput").ap()
    build_from(nc, aps, out)
    r = _run(nc, [arrays], core_ids=[0])
    return r.results[0]["out_dram"]
```

```python
from contextlib import ExitStack

import concourse.bass as bass
from concourse import mybir

F32 = mybir.dt.float32
BF16 = mybir.dt.bfloat16
I32 = mybir.dt.int32
U32 = mybir.dt.uint32
ALU = mybir.AluOpType
ACT = mybir.ActivationFunctionType
AX_X = mybir.AxisListType.X

P = 128
QG = 4
TQ = 8
RQ = 4
NE = 8
HID = 256
PAIRS = [(a, b) for a in range(NE) for b in range(a + 1, NE)]
NPAIR = len(PAIRS)
ROW = P + 5
SECOND = HID + 2
LAST = SECOND + HID
PACK = LAST + P // 2
EPS = 1e-5
ALPHA = 0.2
MASKED = -9.0e15
NEVER = -3.0e38


def build_program(nc, x, adj, gnn_w, gnn_a, gate_w, gate_b, w1, b1, w2, b2, consts, out):
    NG = x.shape[0]
    NQ = NG // QG
    NB = NQ // RQ
    RG = QG * RQ
    NT = NG + NPAIR - 1
    CAP = NG * P + P
    HEADS = (1, gnn_w[1].shape[0])
    MOMENTS = NQ + 5
    SPLIT_LINKS = 5
    N_CONSTS = 7 + len(gate_b) + 2 * HEADS[1]
    ROUTE_LINKS, PLACE_LINKS, PLAN_LINKS, PACK_LINKS = 24, 3, 21, 8
    TB = 2 * P
    assert NT <= TB and NB >= 4 and P % HEADS[1] == 0

    rows_dram = nc.dram_tensor("rows_by_pair", (NPAIR * CAP + P, ROW), F32).ap()
    between = nc.dram_tensor("between_blocks", (NG, P, P), F32).ap()

    with ExitStack() as ctx:
        def sb(name, shape, dt=F32):
            return ctx.enter_context(nc.sbuf_tensor(name, shape, dt))

        def sem(name):
            return ctx.enter_context(nc.semaphore(name))

        X = sb("X", [P, NG, ROW])
        ident = sb("ident", [P, P])
        identb = sb("identb", [P, P], BF16)
        onesb = sb("onesb", [P, P], BF16)
        lower = sb("lower", [P, P], BF16)
        no_row = sb("no_row", [P, ROW])
        adj_i = sb("adj_i", [P, P], I32)
        maskneg = sb("maskneg", [P, P], BF16)
        W = [sb(f"W{l}", [P, P]) for l in range(2)]
        WT = [sb(f"WT{l}", [P, P]) for l in range(2)]
        A = [sb(f"A{l}", [P, 2, HEADS[l]]) for l in range(2)]
        wa1, wa2 = sb("wa1", [P, P]), sb("wa2", [P, P])
        wa = sb("wa", [P, 2 * HEADS[1]])
        Wg = [sb(f"Wg{l}", [P, NE]) for l in range(2)]
        gb_in = sb("gb_in", [P, 3, NE])
        gbias = [sb(f"gbias{l}", [P, NE]) for l in range(2)]
        experts = sb("experts", [P, NE, PACK])

        def two(name, shape, dt=F32):
            return [sb(f"{name}{k}", shape, dt) for k in range(2)]

        mv = [sb(f"mv{k}", [P, 2, QG, 2]) for k in range(RQ)]
        st = [sb(f"st{k}", [P, 2, QG, 6]) for k in range(RQ)]
        shift2 = two("shift2", [P, QG])
        neghalf = sb("neghalf", [P, 2 * QG])
        xn = two("xn", [P, QG, P])
        xnT = two("xnT", [P, QG * P])
        hsb = [sb(f"hsb{k}", [P, QG * P]) for k in range(4)]
        sums = two("sums", [P, QG, 2 * HEADS[1]])
        rest = [sb(f"rest{k}", [P, QG, 2 * HEADS[1]]) for k in range(2)]
        parts = two("parts", [P, QG, P // QG], BF16)
        partsT = two("partsT", [P, P], BF16)
        pick_i = sb("pick_i", [P, QG, HEADS[1], P], BF16)
        pick_j = sb("pick_j", [P, QG, HEADS[1], P], BF16)
        nmx = two("nmx", [P, 4])
        negm = [sb(f"negm{k}", [P, 4]) for k in range(4)]
        rel = two("rel", [P, 4 * P])
        es = two("es", [P, 4 * P])
        ps = two("ps", [P, 4 * P])
        pT = two("pT", [P, 4 * P])
        rowsum = [sb(f"rowsum{k}", [P, QG * max(HEADS)]) for k in range(4)]
        rinv = sb("rinv", [P, QG * max(HEADS)])
        hp = two("hp", [P, QG * P])
        mn = two("mn", [P, QG * P])
        ex = two("ex", [P, QG * P])
        xn2 = two("xn2", [P, QG, P])
        xn2T = two("xn2T", [P, QG * P])

        lg = sb("lg", [P, RG, NE])
        m1 = sb("m1", [P, RG])
        lm = sb("lm", [P, RG, NE])
        EX = sb("EX", [P, RG, NE])
        eq = sb("eq", [P, RG, NE])
        c1 = sb("c1", [P, RG])
        oh = sb("oh", [P, RG, NE])
        lgb = sb("lgb", [P, RG, NE])
        l2 = sb("l2", [P, RG, NE])
        sel = sb("sel", [P, RG, NE])
        tmp8 = sb("tmp8", [P, RG, NE])
        code = sb("code", [P, RG])
        den = sb("den", [P, RG])
        cw = sb("cw", [P, RG, NE])
        cwh = sb("cwh", [P, RG, NE])
        pc = sb("pc", [P, (RG + 1) * NPAIR], BF16)
        slm = sb("slm", [P, RG, NPAIR])
        slotf = sb("slotf", [P, RG])
        base = sb("base", [P, NPAIR])
        idx_rows = [sb(f"idx_rows{l}", [P, NG], U32) for l in range(2)]
        cst = sb("cst", [P, 3 * NE + 5 * NPAIR])
        revidx, pow2, pow2x2 = (cst[:, k * NE:(k + 1) * NE] for k in range(3))
        pairconst, region, grow_region, grow_lower, grow_upper = (
            cst[:, 3 * NE + k * NPAIR:3 * NE + (k + 1) * NPAIR] for k in range(5))
        ones_pair = sb("ones_pair", [P, NPAIR])
        tile_no = sb("tile_no", [P, 2])
        cnt = sb("cnt", [P, NPAIR])
        cnt_i = sb("cnt_i", [P, NPAIR], I32)
        cnt_j = sb("cnt_j", [P, NPAIR], I32)
        wpair = sb("wpair", [P, RG, 2])
        ntile = sb("ntile", [P, NPAIR])
        cum = sb("cum", [P, NPAIR])
        shift = sb("shift", [P, NPAIR])
        le = sb("le", [P, 2, NPAIR])
        lx = sb("lx", [P, 2, NPAIR])
        tvals = sb("tvals", [P, 2, 3])
        tstart = sb("tstart", [P, 2])
        tvalid = sb("tvalid", [P, 2])
        base_i = sb("base_i", [P, NPAIR], I32)
        table = sb("table", [3, TB], I32)

        xs = [sb(f"xs{k}", [P, ROW]) for k in range(TQ)]
        xsn = [sb(f"xsn{k}", [P, P]) for k in range(4)]
        xsT = two("xsT", [P, P])
        weights = sb("weights", [P, 4 * 2 * PACK])
        wst = [weights[:, k * 2 * PACK:(k + 1) * 2 * PACK].rearrange("p (e c) -> p e c", e=2) for k in range(4)]
        b2_rows = weights[0:3, 0:NE * P]
        b2_part = weights[0:3, NE * P:5 * NE * P // 2].bitcast(BF16).rearrange("p (k c) -> p k c", k=3)
        hh = two("hh", [P, 4, P])
        ya = two("ya", [P, P])
        yo = [sb(f"yo{k}", [P, P]) for k in range(4)]

        bank = [ctx.enter_context(nc.psum_tensor(f"bank{k}", [P, 512], F32)) for k in range(8)]
        T_, H_, E_, PT_, O_, G_ = bank[0], bank[1], bank[2:4], bank[4], bank[5:7], bank[7]
        XT_, HH_, Y_ = bank[0:2], bank[2:6], bank[6:8]

        consts_in, consts_dve, consts_pool = sem("consts_in"), sem("consts_dve"), sem("consts_pool")
        setup_pe, setup_act = sem("setup_pe"), sem("setup_act")
        experts_in, b2_in, packed = sem("experts_in"), sem("b2_in"), sem("packed")
        x_in = [sem(f"x_in{j}") for j in range(RQ)]
        stats_done, moments, eps_added, rstd = sem("stats_done"), sem("moments"), sem("eps_added"), sem("rstd")
        xn_ready, xn2_ready, centred2 = sem("xn_ready"), sem("xn2_ready"), sem("centred2")
        xT_done, xT_copied, h_done, h_copied = sem("xT_done"), sem("xT_copied"), sem("h_done"), sem("h_copied")
        s_done, max_done = sem("s_done"), sem("max_done")
        rel_done, e_done, p_done = sem("rel_done"), sem("e_done"), sem("p_done")
        pT_done, pT_copied, o_done = sem("pT_done"), sem("pT_copied"), sem("o_done")
        rinv_done, hp_done, mn_done, ex_done = sem("rinv_done"), sem("hp_done"), sem("mn_done"), sem("ex_done")
        pos_added, resid_done = sem("pos_added"), sem("resid_done")
        x2T_done, x2T_copied, logits_done, lg_done = sem("x2T_done"), sem("x2T_copied"), sem("logits_done"), sem("lg_done")
        route, lm_done, EX_done, pc_done = sem("route"), sem("lm_done"), sem("EX_done"), sem("pc_done")
        ranks_done, slots_done, scattered = sem("ranks_done"), sem("slots_done"), sem("scattered")
        plan, tvals_done, tableT_done, table_done = sem("plan"), sem("tvals_done"), sem("tableT_done"), sem("table_done")
        padded, absorbed = sem("padded"), sem("absorbed")
        staged_upper = sem("staged_upper")
        xs_in = [sem(f"xs_in{k}") for k in range(TQ)]
        xsn_done, staged, xsT_done, xsT_copied = sem("xsn_done"), sem("staged"), sem("xsT_done"), sem("xsT_copied")
        hh_done, act_done, y_done, ya_done, yo_done = sem("hh_done"), sem("act_done"), sem("y_done"), sem("ya_done"), sem("yo_done")
        y_out = [sem(f"y_out{k}") for k in range(4)]
        base_reset, placing = sem("base_reset"), sem("placing")
        sums_done, sums_copied, split = sem("sums_done"), sem("sums_copied"), sem("split")
        partsT_done, partsT_copied = sem("partsT_done"), sem("partsT_copied")
        centred, shifted, shift2_done = sem("centred"), sem("shifted"), sem("shift2_done")

        block = ctx.enter_context(nc.Block())

        def attention_steps(eng, step, tail):
            for t in range(3 * RQ):
                step(t, t % RQ, t // RQ)
            with eng.Fori(3, NB) as b:
                for j in range(RQ):
                    step(b * RQ + j, j, b)
            for t in range(NQ, NQ + tail):
                step(t, t % RQ, t // RQ)

        def tile_steps(eng, step, tail):
            for t in range(TQ):
                step(t, t % TQ, 0)
            with eng.Fori(1, NT // TQ) as b:
                for j in range(TQ):
                    step(b * TQ + j, j, b)
            for t in range(NT // TQ * TQ, NT + tail):
                step(t, t % TQ, t // TQ)

        def in_slot(k, n):
            return (NT - k + n - 1) // n

        def there(t, lag, n):
            return not isinstance(t, int) or 0 <= t - lag < n

        def later(l, t, j, B):
            return (t - 1, (j - 1) % RQ, B - 1 if j == 0 else B) if l else (t, j, B)

        def wait(eng, s, value):
            if not isinstance(value, int) or value > 0:
                eng.wait_ge(s, value)

        UNITS = (1, QG)
        BEHIND = (dict(scores=-1, leaky=0, exps=0, turn=1, mix=1), dict(scores=-1, leaky=1, exps=1, turn=2, mix=3))

        def unit(l, t, j, u, stage):
            at = u - BEHIND[l][stage] if stage else u
            steps_back = 2 + l - at // UNITS[l]
            u = at % UNITS[l]
            q = t - steps_back
            return q, (j - steps_back) % 4, u, (q if l == 0 else NQ + q * QG + u), there(t, steps_back, NQ)

        def xcols(q, lo, hi):
            if isinstance(q, int):
                return X[:, QG * q:QG * q + QG, lo:hi]
            return X[:, bass.ds(q * QG, QG), lo:hi]

        def graph(q, g, lo, hi):
            if isinstance(q, int):
                return X[:, QG * q + g, lo:hi]
            return X[:, bass.ds(q * QG + g, 1), lo:hi].rearrange("p a d -> p (a d)")

        def of_batch(t, b):
            if isinstance(b, int):
                return t[:, RG * b:RG * b + RG]
            return t[:, bass.ds(b * RG, RG)]

        def each(t, n):
            return t.unsqueeze(2).to_broadcast([P, t.shape[1], n])

        def along(t, k):
            return t.unsqueeze(1).to_broadcast([P, k, t.shape[1]])

        def zero_ends(eng, pairs):
            for c in pairs:
                end = eng.value_load(base_i[0:1, c:c + 1], min_val=0, max_val=NPAIR * CAP - P)
                eng.dma_start(rows_dram[bass.ds(end, P), :], no_row[:, :]).then_inc(padded, 16)

        @block.sync
        def _(sp):
            loads = [(adj_i[:, :], adj), (W[0][:, :], gnn_w[0]),
                     (W[1][:, :].rearrange("p (h d) -> p h d", h=HEADS[1]), gnn_w[1].rearrange("h f d -> f h d")),
                     (Wg[0][:, :], gate_w[0]), (Wg[1][:, :], gate_w[1]),
                     (A[0][:, :, :].rearrange("p c h -> p (c h)"), gnn_a[0].rearrange("(c p) h -> p (c h)", c=2)),
                     (cst[:, :], consts.partition_broadcast(P))]
            for k, v in enumerate(gate_b):
                loads.append((gb_in[:, k, :], v.partition_broadcast(P)))
            for dst, src in loads:
                sp.dma_start(dst, src, allow_slow_non_contiguous=True).then_inc(consts_in, 16)
            sp.wait_ge(consts_pool, 1)
            hs = P // HEADS[1]
            for h in range(HEADS[1]):
                for c in range(2):
                    sp.dma_start(A[1][h * hs:(h + 1) * hs, c, h:h + 1],
                                 gnn_a[1][h:h + 1, c * hs:(c + 1) * hs].rearrange("a d -> d a"),
                                 allow_slow_non_contiguous=True).then_inc(consts_in, 16)

            def load_x(t, j, B):
                wait(sp, x_in[j], (B + l * NB) * 16)
                src = (between if l else x)
                src = src[QG * t:QG * t + QG] if isinstance(t, int) else src[bass.ds(t * QG, QG)]
                sp.dma_start(xcols(t, 0, P), src.rearrange("g p d -> p g d")).then_inc(x_in[j], 16)

            for l in range(2):
                attention_steps(sp, load_x, 0)

                if l == 0:
                    sp.wait_ge(consts_pool, 4)
                    sp.dma_start(rows_dram[NPAIR * CAP:NPAIR * CAP + P], no_row[:, :]).then_inc(padded, 16)
                else:
                    sp.wait_ge(staged, NT)
                    sp.wait_ge(staged_upper, NT)
                for e in range(NE):
                    sp.dma_start(experts[:, e, 0:HID], w1[l][e]).then_inc(experts_in, 16)
                    sp.dma_start(experts[:, e, SECOND:LAST].rearrange("p (c d) -> p c d", c=2),
                                 w2[l][e].rearrange("(c p) d -> p c d", c=2)).then_inc(experts_in, 16)
                    sp.dma_start(experts[:, e, HID:SECOND],
                                 b1[l][e].rearrange("(c p) -> p c", c=2),
                                 allow_slow_non_contiguous=True).then_inc(experts_in, 16)
                sp.dma_start(b2_rows[:, :], b2[l].rearrange("e d -> (e d)").partition_broadcast(3)).then_inc(b2_in, 16)

                sp.wait_ge(plan, l * PLAN_LINKS + 1)
                zero_ends(sp, range(0, NPAIR, 2))
                sp.wait_ge(scattered, 16 * NG * (l + 1))
                sp.wait_ge(padded, 16 * (NPAIR * (l + 1) + 1))
                sp.wait_ge(table_done, l + 1)

                def load_rows(t, j, b):
                    if there(t, 0, NT):
                        col = slice(t, t + 1) if isinstance(t, int) else bass.ds(t, 1)
                        row = sp.value_load(table[0:1, col], min_val=0, max_val=NPAIR * CAP)
                        if there(t, TQ, NT):
                            sp.wait_ge(y_out[j % 4], (b * 2 + (j // 4 - 1 + in_slot(j % 4, 4) * l)) * 16)
                        sp.dma_start(xs[j][:, :], rows_dram[bass.ds(row, P), :]).then_inc(xs_in[j], 16)

                tile_steps(sp, load_rows, 0)
                for k in range(4):
                    sp.wait_ge(y_out[k], 16 * in_slot(k, 4) * (l + 1))

        @block.gpsimd
        def _(pool):
            pool.memset(A[1][:, :, :], 0.0).then_inc(consts_pool, 1)
            pool.memset(experts[:, :, LAST:PACK], 0.0).then_inc(consts_pool, 1)
            pool.memset(onesb[:, :], 1.0)
            pool.memset(no_row[:, 0:ROW - 1], 0.0)
            pool.iota(no_row[:, ROW - 1:ROW].bitcast(I32), [[0, 1]], base=NG * P, channel_multiplier=1)
            pool.iota(X[:, :, ROW - 1:ROW].bitcast(I32).rearrange("p n a -> p (n a)"), [[P, NG]], base=0,
                      channel_multiplier=1)
            pool.memset(ones_pair[:, :], 1.0)
            pool.memset(neghalf[:, :], -0.5)
            pool.memset(pc[:, :], 0.0)
            for k in range(2):
                pool.memset(parts[k][:, :, :], 0.0)
            pool.iota(tile_no[:, :], [[P, 2]], base=0, channel_multiplier=1, allow_small_or_imprecise_dtypes=True)
            pool.memset(lower[:, :], 0.0)
            pool.memset(identb[:, :], 0.0)
            pool.memset(ident[:, :], 0.0).then_inc(consts_pool, 1)
            pool.wait_ge(consts_pool, 3)
            pool.affine_select(out=ident[:, :], in_=ident[:, :], compare_op=ALU.not_equal, fill=1.0, base=0,
                               pattern=[[-1, P]], channel_multiplier=1)
            pool.affine_select(out=identb[:, :], in_=identb[:, :], compare_op=ALU.not_equal, fill=1.0, base=0,
                               pattern=[[-1, P]], channel_multiplier=1)
            pool.affine_select(out=lower[:, :], in_=lower[:, :], compare_op=ALU.is_ge, fill=1.0, base=0,
                               pattern=[[-1, P]], channel_multiplier=1).then_inc(consts_pool, 1)

            def pool_held(s, value):
                if not isinstance(value, int) or value > 0:
                    pool.wait_ge(s, value)
                    pool.sem_inc(absorbed, 1)

            def deviations(l, t, lo, hi):
                n = l * MOMENTS + t + 1
                var = mv[t % RQ][:, lo:hi, :, 1].rearrange("p n g -> p (n g)")
                pool.wait_ge(moments, n)
                pool.tensor_scalar(var, var, EPS, None, ALU.add).then_inc(eps_added, 1)
                pool.wait_ge(eps_added, n)
                pool.tensor_tensor(var, var, neghalf[:, 0:(hi - lo) * QG], ALU.pow).then_inc(rstd, 1)
                pool.wait_ge(rstd, n)

            def normalise(n, m, q, xn_, centred_, n_centred, ready, used):
                wait(pool, used, n - 2)
                pool.tensor_tensor(xn_[:, :, :], X[:, QG * q:QG * q + QG, 0:P], each(m[:, :, 0], P),
                                   ALU.subtract).then_inc(centred_, 1)
                pool.wait_ge(centred_, n_centred)
                pool.tensor_tensor(xn_[:, :, :], xn_[:, :, :], each(m[:, :, 1], P), ALU.mult).then_inc(ready, 1)

            def row_moments(l, q, m):
                n = l * NQ + q + 1
                pool.tensor_copy(X[:, QG * q:QG * q + QG, P:P + 2], m)
                if l:
                    normalise(n, m, q, xn2[q % 2], centred2, q + 1, xn2_ready, x2T_done)
                    return
                pool.tensor_tensor(shift2[q % 2][:, :], m[:, :, 0], m[:, :, 1], ALU.mult).then_inc(shifted, 1)
                pool.wait_ge(shifted, n)
                pool.tensor_scalar(shift2[q % 2][:, :], shift2[q % 2][:, :], -1.0, None,
                                   ALU.mult).then_inc(shift2_done, 1)

            def split_sums(q):
                pool.wait_ge(sums_copied, q + 1)
                wait(pool, partsT_done, q - 1)
                n = 2 * HEADS[1]
                left = sums[q % 2][:, :, :]
                for k in range(3):
                    part = parts[q % 2][:, :, k * n:(k + 1) * n]
                    pool.tensor_copy(part, left).then_inc(split, 1)
                    pool.wait_ge(split, q * SPLIT_LINKS + 2 * k + 1)
                    if k < 2:
                        pool.tensor_tensor(rest[k][:, :, :], left, part, ALU.subtract).then_inc(split, 1)
                        pool.wait_ge(split, q * SPLIT_LINKS + 2 * k + 2)
                        left = rest[k][:, :, :]

            for l in range(2):
                for t in range(NQ + 15 + l):
                    if l and 0 <= t - 2 < NQ:
                        split_sums(t - 2)
                    first, second = t < NQ, 0 <= t - 5 - l < NQ
                    if first or second:
                        deviations(l, t, 0 if first else 1, 2 if second else 1)
                    if second:
                        row_moments(l, t - 5 - l, mv[t % RQ][:, 1, :, :])
                    if first:
                        normalise(l * NQ + t + 1, mv[t % RQ][:, 0, :, :], t, xn[t % 2], centred, l * NQ + t + 1,
                                  xn_ready, xT_done)
                    b, part = divmod(t - 15 - l, RQ)
                    if 0 <= b < NB:
                        pool.wait_ge(slots_done, l * NB + b + 1)
                        for n in range(RG * b + QG * part, RG * b + QG * part + QG):
                            pool.indirect_dma_start(rows_dram,
                                                    bass.IndirectOffsetOnAxis(ap=idx_rows[l][:, n:n + 1], axis=0),
                                                    X[:, n, :], None).then_inc(scattered, 16)

                pool.wait_ge(table_done, l + 1)
                if l == 0:
                    for pick, c in ((pick_i, 0), (pick_j, HEADS[1])):
                        pool.memset(pick[:, :, :, :], 0.0).then_inc(consts_pool, 1)
                        for k in range(3):
                            pool.wait_ge(consts_pool, 5 + 4 * (c > 0) + k)
                            pool.affine_select(out=pick[:, :, :, :], in_=pick[:, :, :, :], compare_op=ALU.not_equal,
                                               fill=1.0, base=-(2 * HEADS[1] * k + c), channel_multiplier=1,
                                               pattern=[[-(P // QG), QG], [-1, HEADS[1]], [0, P]]
                                               ).then_inc(consts_pool, 1)
                result = (out if l else between).rearrange("g p d -> (g p) d")

                def store_rows(t, j, b):
                    if there(t, 0, NT):
                        pool_held(yo_done, NT * l + t + 1)
                        pool.indirect_dma_start(result, bass.IndirectOffsetOnAxis(
                            ap=xs[j][:, ROW - 1:ROW].bitcast(U32), axis=0), yo[j % 4][:, :], None,
                            bounds_check=NG * P - 1, oob_is_err=False).then_inc(y_out[j % 4], 16)

                tile_steps(pool, store_rows, 0)

        @block.tensor
        def _(pe):
            pe.wait_ge(consts_pool, 4)
            pe.wait_ge(consts_in, 16 * N_CONSTS)
            for l in range(2):
                mm = pe.transpose(bank[l][:, 0:P], W[l][:, :], ident[:, :])
            mm.then_inc(setup_pe, 1)
            pe.wait_ge(setup_act, 2)
            for c in range(2):
                pe.matmul(bank[2 + c][:, 0:P], WT[0][:, :], A[0][:, c, :].to_broadcast([P, P]), start=True, stop=True)
            pe.matmul(bank[4][:, 0:2 * HEADS[1]], WT[1][:, :], A[1][:, :, :].rearrange("p c h -> p (c h)"),
                      start=True, stop=True).then_inc(setup_pe, 1)
            pe.wait_ge(setup_act, 5)
            pe.wait_ge(consts_dve, 3)

            for l in range(2):
                H = HEADS[l]
                hs = P // H

                def transposes(t, j):
                    if not there(t, 1, NQ):
                        return
                    if there(t, 7, NQ):
                        pe.wait_ge(x2T_copied, l * NQ + t - 6)
                    elif l:
                        wait(pe, sums_copied, t - 1)
                    pe.wait_ge(xn_ready, l * NQ + t)
                    for g in range(QG):
                        mm = pe.transpose(T_[:, g * P:(g + 1) * P], xn[(j - 1) % 2][:, g, :], ident[:, :])
                    mm.then_inc(xT_done, 1)

                def project(t, j):
                    if not there(t, 1, NQ):
                        return
                    G = l * NQ + t - 1
                    wait(pe, h_copied, G)
                    pe.wait_ge(xT_copied, G + 1)
                    for g in range(QG):
                        mm = pe.matmul(H_[:, g * P:(g + 1) * P], xnT[(j - 1) % 2][:, g * P:(g + 1) * P], W[l][:, :],
                                       start=True, stop=True)
                    mm.then_inc(h_done, 1)

                def summands(t, j):
                    if not there(t, 1, NQ):
                        return
                    for g in range(QG):
                        mm = pe.matmul(T_[:, g * 2 * H:(g + 1) * 2 * H], xnT[(j - 1) % 2][:, g * P:(g + 1) * P],
                                       wa[:, :], start=True, stop=True)
                    mm.then_inc(sums_done, 1)

                def turn_parts(t, j):
                    if not there(t, 2, NQ):
                        return
                    if not there(t, 1, NQ):
                        pe.wait_ge(x2T_copied, l * NQ + t - 6)
                    pe.wait_ge(split, (t - 1) * SPLIT_LINKS)
                    pe.transpose(T_[:, 3 * P:4 * P].bitcast(BF16)[:, 0:P], parts[j % 2][:, :, :].rearrange(
                        "p g c -> p (g c)"), identb[:, :]).then_inc(partsT_done, 1)

                def scores(t, j, u0):
                    q, ph, u, n, exists = unit(l, t, j, u0, "scores")
                    if not exists:
                        return
                    e = E_[ph % 2 if l == 0 else u % 2]
                    wait(pe, e_done, n - 1)
                    if l and u == 0:
                        pe.wait_ge(partsT_copied, q + 1)
                    pe.matmul(e[:, :], identb[:, :], along(maskneg[:, :], 4), start=True, stop=False)
                    if l == 0:
                        xT = xnT[ph % 2]
                        pe.matmul(e[:, :], wa2[:, :], xT[:, :], start=False, stop=False)
                        for g in range(QG):
                            mm = pe.matmul(e[:, g * P:(g + 1) * P], xT[:, g * P:(g + 1) * P], wa1[:, :],
                                           start=False, stop=(g == QG - 1))
                    else:
                        pT_ = partsT[ph % 2]
                        pe.matmul(e[:, :], pT_[:, :], pick_i[:, u, :, :].rearrange("p h i -> p (h i)"),
                                  start=False, stop=False)
                        for h in range(H):
                            mm = pe.matmul(e[:, h * P:(h + 1) * P], pick_j[:, u, h, :], pT_[:, :],
                                           start=False, stop=(h == H - 1))
                    mm.then_inc(s_done, 1)

                def turn(t, j, u0):
                    q, ph, u, n, exists = unit(l, t, j, u0, "turn")
                    if not exists:
                        return
                    k = ph % 2 if l == 0 else u % 2
                    if l:
                        wait(pe, pT_copied, n)
                    pe.wait_ge(p_done, n + 1)
                    for i in range(4):
                        mm = pe.transpose(PT_[:, i * P:(i + 1) * P], ps[k][:, i * P:(i + 1) * P], ident[:, :])
                    mm.then_inc(pT_done, 1)

                def mix(t, j, u0):
                    q, ph, u, n, exists = unit(l, t, j, u0, "mix")
                    if not exists:
                        return
                    G = l * NQ + q
                    k = ph % 2 if l == 0 else u % 2
                    if u == 0:
                        pe.wait_ge(h_copied, G + 1)
                        wait(pe, hp_done, G - 1)
                    pe.wait_ge(pT_copied, n + 1)
                    for i in range(4):
                        p_i = pT[k][:, i * P:(i + 1) * P]
                        if l == 0:
                            c = slice(i * P, (i + 1) * P)
                        else:
                            c = slice(u * P + i * hs, u * P + (i + 1) * hs)
                        mm = pe.matmul(O_[ph % 2][:, c], p_i, hsb[ph][:, c], start=True, stop=True)
                    mm.then_inc(o_done, 1)

                def transposes2(t, j):
                    if not there(t, 6, NQ):
                        return
                    if l:
                        pe.wait_ge(sums_copied, min(t, NQ) if isinstance(t, int) else t)
                    pe.wait_ge(xn2_ready, l * NQ + t - 5)
                    for g in range(QG):
                        mm = pe.transpose(T_[:, g * P:(g + 1) * P], xn2[j % 2][:, g, :], ident[:, :])
                    mm.then_inc(x2T_done, 1)

                def logits(t, j, B):
                    lag = 7 - l
                    if not there(t, lag, NQ):
                        return
                    G = l * NQ + t - lag
                    wait(pe, lg_done, G)
                    if j == 3 - l and not (isinstance(t, int) and B < 3):
                        pe.wait_ge(slots_done, l * NB + B - 2)
                    pe.wait_ge(x2T_copied, G + 1)
                    for g in range(QG):
                        mm = pe.matmul(G_[:, 480 + g * NE:480 + (g + 1) * NE],
                                       xn2T[(j - lag) % 2][:, g * P:(g + 1) * P], Wg[l][:, :], start=True, stop=True)
                    mm.then_inc(logits_done, 1)

                def ranks(t, j, B):
                    if j != 2 or not there(t, 14, NQ):
                        return
                    width = (RG + 1) * NPAIR
                    pe.wait_ge(pc_done, l * NB + B - 2)
                    pe.wait_ge(lg_done, l * NQ + (min(t - 6, NQ) if isinstance(t, int) else t - 6))
                    pe.matmul(G_[:, 0:width], lower[:, :], pc[:, :], start=True, stop=False)
                    for s in range(1, RG + 1):
                        mm = pe.matmul(G_[:, s * NPAIR:width], onesb[:, :], pc[:, 0:width - s * NPAIR],
                                       start=False, stop=(s == RG))
                    mm.then_inc(ranks_done, 1)

                def step(t, j, B):
                    if l == 0:
                        turn(t, j, 0)
                        transposes(t, j)
                        logits(t, j, B)
                        mix(t, j, 0)
                        project(t, j)
                        scores(t, j, 0)
                        ranks(t, j, B)
                        transposes2(t, j)
                    else:
                        late = later(l, t, j, B)
                        for u in range(4):
                            if u < 3:
                                scores(t, j, u)
                            turn(t, j, u)
                            if u == 0:
                                transposes2(*late[0:2])
                                ranks(*late)
                            elif u == 1:
                                transposes(t, j)
                            elif u == 2:
                                project(t, j)
                                summands(t, j)
                                turn_parts(t, j)
                            else:
                                scores(t, j, u)
                                logits(*late)
                            mix(t, j, u)

                if l:
                    pe.wait_ge(consts_pool, 12)
                attention_steps(pe, step, 11 + l)

                pe.wait_ge(tvals_done, l + 1)
                for c in range(2):
                    mm = pe.transpose(T_[0:3, c * P:(c + 1) * P], tvals[:, c, :], ident[:, :])
                mm.then_inc(tableT_done, 1)

                def tile(t, j, b):
                    T = NT * l + t
                    if there(t, 0, NT):
                        pe.wait_ge(xsn_done, T + 1)
                        pe.transpose(XT_[j % 2][:, 0:P], xsn[j % 4][:, :], ident[:, :]).then_inc(xsT_done, 1)
                    if there(t, 1, NT):
                        k = (j - 1) % 4
                        pe.wait_ge(staged, T)
                        pe.wait_ge(staged_upper, T)
                        pe.wait_ge(xsT_copied, T)
                        for c in range(4):
                            mm = pe.matmul(HH_[k][:, c * P:(c + 1) * P],
                                           wst[k][:, c // 2, (c % 2) * P:(c % 2 + 1) * P], xsT[k % 2][:, :],
                                           start=True, stop=True)
                        mm.then_inc(hh_done, 1)
                    if there(t, 2, NT):
                        k = (j - 2) % 4
                        wait(pe, yo_done, T - 3)
                        pe.wait_ge(act_done, T - 1)
                        pe.matmul(Y_[k % 2][:, 0:2 * P], onesb[0:3, :], wst[k][0:3, :, LAST:PACK].bitcast(BF16),
                                  start=True, stop=False)
                        for e in range(2):
                            y = Y_[k % 2][:, e * P:(e + 1) * P]
                            for c in range(2):
                                mm = pe.matmul(y, hh[k % 2][:, 2 * e + c, :],
                                               wst[k][:, e, SECOND + c * P:SECOND + (c + 1) * P],
                                               start=False, stop=(e == c == 1))
                        mm.then_inc(y_done, 1)

                tile_steps(pe, tile, 2)

        @block.scalar
        def _(act):
            act.preload_act_table_set("exp_and_others")
            act.wait_ge(setup_pe, 1)
            for l in range(2):
                act.activation(WT[l][:, :], bank[l][:, 0:P], ACT.Copy).then_inc(setup_act, 1)
            act.wait_ge(setup_pe, 2)
            for c, repeated in enumerate((wa1, wa2)):
                act.activation(repeated[:, :], bank[2 + c][:, 0:P], ACT.Copy).then_inc(setup_act, 1)
            act.activation(wa[:, :], bank[4][:, 0:2 * HEADS[1]], ACT.Copy).then_inc(setup_act, 1)

            for l in range(2):
                H = HEADS[l]

                def copy_xT(t, j):
                    if there(t, 1, NQ):
                        act.wait_ge(xT_done, l * NQ + t)
                        act.activation(xnT[(j - 1) % 2][:, :], T_[:, :], ACT.Copy).then_inc(xT_copied, 1)

                def copy_sums(t, j):
                    if there(t, 1, NQ):
                        act.wait_ge(sums_done, t)
                        act.activation(sums[(j - 1) % 2][:, :, :].rearrange("p g c -> p (g c)"), T_[:, 0:QG * 2 * H],
                                       ACT.Copy).then_inc(sums_copied, 1)

                def copy_partsT(t, j):
                    if there(t, 2, NQ):
                        act.wait_ge(partsT_done, t - 1)
                        act.activation(partsT[j % 2][:, :], T_[:, 3 * P:4 * P].bitcast(BF16)[:, 0:P],
                                       ACT.Copy).then_inc(partsT_copied, 1)

                def copy_h(t, j):
                    if there(t, 1, NQ):
                        act.wait_ge(h_done, l * NQ + t)
                        act.activation(hsb[(j - 1) % 4][:, :], H_[:, :], ACT.Copy).then_inc(h_copied, 1)

                def rectify(t, j, u0):
                    q, ph, u, n, exists = unit(l, t, j, u0, None)
                    if exists:
                        k = ph % 2 if l == 0 else u % 2
                        act.wait_ge(max_done, n + 1)
                        act.activation(rel[k][:, :], E_[k][:, :], ACT.Relu, scale=1.0 - ALPHA).then_inc(rel_done, 1)

                def exps(t, j, u0):
                    q, ph, u, n, exists = unit(l, t, j, u0, "exps")
                    if exists:
                        k = ph % 2 if l == 0 else u % 2
                        act.wait_ge(e_done, n + 1)
                        for i in range(4):
                            ins = act.activation(ps[k][:, i * P:(i + 1) * P], es[k][:, i * P:(i + 1) * P], ACT.Exp,
                                                 bias=negm[ph if l == 0 else u][:, i:i + 1],
                                                 accum_out=rowsum[ph][:, 4 * u + i:4 * u + i + 1])
                        ins.then_inc(p_done, 1)

                def copy_pT(t, j, u0):
                    q, ph, u, n, exists = unit(l, t, j, u0, "turn")
                    if exists:
                        k = ph % 2 if l == 0 else u % 2
                        act.wait_ge(pT_done, n + 1)
                        act.activation(pT[k][:, :], PT_[:, :], ACT.Copy).then_inc(pT_copied, 1)

                def negated_min(t, j):
                    if there(t, 4, NQ):
                        act.wait_ge(hp_done, l * NQ + t - 3)
                        act.activation(mn[j % 2][:, :], hp[j % 2][:, :], ACT.Relu, scale=-1.0).then_inc(mn_done, 1)

                def exp_neg(t, j):
                    if there(t, 4, NQ):
                        act.wait_ge(mn_done, l * NQ + t - 3)
                        act.activation(ex[j % 2][:, :], mn[j % 2][:, :], ACT.Exp,
                                       scale=1.0 if l else -1.0).then_inc(ex_done, 1)

                def normalise2(t, j):
                    if there(t, 6, NQ):
                        k = j % 2
                        act.wait_ge(shift2_done, l * NQ + t - 5)
                        for g in range(QG):
                            ins = act.activation(xn2[k][:, g, :], graph(t - 6, g, 0, P), ACT.Identity,
                                                 bias=shift2[k][:, g:g + 1], scale=mv[(j - 1) % RQ][:, 1, g, 1:2])
                        ins.then_inc(xn2_ready, 1)

                def copy_x2T(t, j):
                    if there(t, 6, NQ):
                        act.wait_ge(x2T_done, l * NQ + t - 5)
                        act.activation(xn2T[j % 2][:, :], T_[:, :], ACT.Copy).then_inc(x2T_copied, 1)

                def exp_logits(t, j, B):
                    if j == 3 and there(t, 11, NQ):
                        act.wait_ge(lm_done, l * NB + B - 1)
                        act.activation(EX[:, :, :], lm[:, :, :], ACT.Exp).then_inc(EX_done, 1)

                def step(t, j, B):
                    if l == 0:
                        copy_pT(t, j, 0)
                        copy_xT(t, j)
                        rectify(t, j, 0)
                        negated_min(t, j)
                        normalise2(t, j)
                        exp_neg(t, j)
                        copy_h(t, j)
                        exps(t, j, 0)
                        copy_x2T(t, j)
                        exp_logits(t, j, B)
                    else:
                        late = later(l, t, j, B)
                        for u in range(4):
                            rectify(t, j, u)
                            exps(t, j, u)
                            copy_pT(t, j, u)
                            if u == 0:
                                copy_x2T(*late[0:2])
                            elif u == 1:
                                copy_xT(t, j)
                            elif u == 2:
                                exp_neg(*late[0:2])
                                copy_partsT(t, j)
                            else:
                                copy_sums(t, j)
                                copy_h(t, j)
                                exp_logits(*late)

                attention_steps(act, step, 8 + l)
                if l:
                    act.preload_act_table_set("gelu_and_others")
                act.wait_ge(plan, l * PLAN_LINKS + 1)
                zero_ends(act, range(1, NPAIR, 2))
                func = ACT.Gelu if l else ACT.Relu
                act.wait_ge(experts_in, 16 * 3 * NE * (l + 1))
                act.wait_ge(packed, (l + 1) * PACK_LINKS)
                act.wait_ge(table_done, l + 1)

                def tile(t, j, b):
                    T = NT * l + t
                    if there(t, 0, NT):
                        col = slice(t, t + 1) if isinstance(t, int) else bass.ds(t, 1)
                        expert = act.value_load(table[2:3, col], min_val=0, max_val=NE - 1)
                        act.activation(wst[j % 4][:, 1, :], experts[:, bass.ds(expert, 1), :].rearrange(
                            "p a c -> p (a c)"), ACT.Copy).then_inc(staged_upper, 1)
                        act.wait_ge(xsT_done, T + 1)
                        act.activation(xsT[j % 2][:, :], XT_[j % 2][:, 0:P], ACT.Copy).then_inc(xsT_copied, 1)
                    if there(t, 1, NT):
                        k = (j - 1) % 4
                        act.wait_ge(hh_done, T)
                        for c in range(4):
                            ins = act.activation(hh[k % 2][:, c, :], HH_[k][:, c * P:(c + 1) * P], func,
                                                 bias=wst[k][:, c // 2, HID + c % 2:HID + c % 2 + 1])
                        ins.then_inc(act_done, 1)

                tile_steps(act, tile, 1)
                if l == 0:
                    act.preload_act_table_set("exp_and_others")

        @block.vector
        def _(dve):
            def linker(s, before, links):
                done = [0]

                def run(ins):
                    done[0] += 1
                    assert done[0] <= links
                    ins.then_inc(s, 1)
                    dve.wait_ge(s, before + done[0])
                return run

            def held(s, value):
                dve.wait_ge(s, value)
                dve.sem_inc(absorbed, 1)

            dve.wait_ge(consts_in, 16 * N_CONSTS)
            dve.tensor_scalar(maskneg[:, :], adj_i[:, :], 0, MASKED, ALU.is_le, ALU.mult).then_inc(consts_dve, 1)
            dve.tensor_tensor(gbias[0][:, :], gb_in[:, 0, :], gb_in[:, 1, :], ALU.add).then_inc(consts_dve, 1)
            dve.tensor_copy(gbias[1][:, :], gb_in[:, 2, :]).then_inc(consts_dve, 1)
            dve.wait_ge(consts_pool, 4)

            for l in range(2):
                H = HEADS[l]

                def norm_moments(t, j, B):
                    back = 5 + l
                    norms = [(0, t)] * there(t, 0, NQ) + [(1, t - back)] * there(t, back, NQ)
                    if not norms:
                        return
                    if there(t, 0, NQ):
                        held(x_in[j], (B + (l * NB + 1)) * 16)
                    if there(t, back, NQ):
                        held(resid_done, l * NQ + t - back + 1)
                    for i, q in norms:
                        for g in range(QG):
                            ins = dve.bn_stats(st[j][:, i, g, :], graph(q, g, 0, P))
                    ins.then_inc(stats_done, 1)
                    held(stats_done, l * MOMENTS + t + 1)
                    for i, q in norms:
                        for g in range(QG):
                            ins = dve.bn_aggr(mv[j][:, i, g, :], st[j][:, i, g, :])
                    ins.then_inc(moments, 1)

                def maxima(t, j, u0):
                    q, ph, u, n, exists = unit(l, t, j, u0, None)
                    if not exists:
                        return
                    k = ph % 2 if l == 0 else u % 2
                    dve.wait_ge(s_done, n + 1)
                    dve.tensor_reduce(nmx[k][:, :], E_[k][:, :].rearrange("p (b c) -> p b c", b=4), AX_X, ALU.max,
                                      negate=True).then_inc(max_done, 1)

                def negated_leaky_max(t, j, u0):
                    q, ph, u, n, exists = unit(l, t, j, u0, None)
                    if not exists:
                        return
                    k = ph % 2 if l == 0 else u % 2
                    dve.wait_ge(max_done, n + 1)
                    dve.scalar_tensor_tensor(negm[ph if l == 0 else u][:, :], nmx[k][:, :], ALPHA, nmx[k][:, :],
                                             ALU.mult, ALU.min)

                def leaky(t, j, u0):
                    q, ph, u, n, exists = unit(l, t, j, u0, "leaky")
                    if not exists:
                        return
                    k = ph % 2 if l == 0 else u % 2
                    dve.wait_ge(rel_done, n + 1)
                    dve.scalar_tensor_tensor(es[k][:, :], E_[k][:, :], ALPHA, rel[k][:, :], ALU.mult,
                                             ALU.add).then_inc(e_done, 1)

                def invert_sums(t, j):
                    if not there(t, 4, NQ):
                        return
                    dve.wait_ge(o_done, t - 3 if l == 0 else NQ + (t - 3) * QG)
                    dve.reciprocal(rinv[:, 0:QG * H], rowsum[j][:, 0:QG * H]).then_inc(rinv_done, 1)

                def weigh(t, j):
                    if not there(t, 4, NQ):
                        return
                    G = l * NQ + t - 4
                    k = j % 2
                    dve.wait_ge(rinv_done, G + 1)
                    dve.tensor_tensor(hp[k][:, :].rearrange("p (b c) -> p b c", b=QG * H),
                                      O_[j % 2][:, :].rearrange("p (b c) -> p b c", b=QG * H),
                                      each(rinv[:, 0:QG * H], P // H), ALU.mult).then_inc(hp_done, 1)
                    if l:
                        dve.wait_ge(hp_done, G + 1)
                        dve.tensor_scalar(mn[k][:, :], hp[k][:, :], 0.0, None, ALU.min).then_inc(mn_done, 1)

                def add_positive(t, j):
                    if not there(t, 4, NQ):
                        return
                    k = j % 2
                    dve.wait_ge(mn_done, l * NQ + t - 3)
                    h3 = hp[k][:, :].rearrange("p (g d) -> p g d", g=QG)
                    dve.scalar_tensor_tensor(h3, h3, 0.0, xcols(t - 4, 0, P), ALU.max, ALU.add).then_inc(pos_added, 1)

                def residual(t, j):
                    if not there(t, 4, NQ):
                        return
                    G = l * NQ + t - 4
                    k = j % 2
                    h3 = hp[k][:, :].rearrange("p (g d) -> p g d", g=QG)
                    dve.wait_ge(pos_added, G + 1)
                    dve.wait_ge(ex_done, G + 1)
                    dve.scalar_tensor_tensor(xcols(t - 4, 0, P), ex[k][:, :].rearrange("p (g d) -> p g d", g=QG), -1.0,
                                             h3, ALU.add, ALU.add).then_inc(resid_done, 1)

                def take_logits(t, j):
                    if not there(t, 7, NQ):
                        return
                    ph = (j - 7) % 4
                    dve.wait_ge(logits_done, l * NQ + t - 6)
                    dve.tensor_tensor(lg[:, QG * ph:QG * ph + QG, :],
                                      G_[:, 480:480 + QG * NE].rearrange("p (g e) -> p g e", g=QG),
                                      along(gbias[l][:, :], QG), ALU.add).then_inc(lg_done, 1)

                def first_of(link, values, peak, onehot):
                    link(dve.tensor_tensor(eq[:, :, :], values, each(peak, NE), ALU.is_equal))
                    link(dve.tensor_tensor(eq[:, :, :], eq[:, :, :], along(revidx, RG), ALU.mult))
                    link(dve.tensor_reduce(c1[:, :], eq[:, :, :], AX_X, ALU.max))
                    link(dve.tensor_tensor(onehot, eq[:, :, :], each(c1[:, :], NE), ALU.is_equal))

                def choose(t, j, B):
                    V = dve
                    back = 2 if j >= 2 else 3
                    if not there(t, {2: 10, 3: 11, 0: 12, 1: 13}[j], NQ):
                        return
                    b = B - back
                    N = l * NB + b
                    done = {2: 0, 3: 6, 0: 12, 1: 17}[j]
                    link = linker(route, N * ROUTE_LINKS + done, ROUTE_LINKS - done)
                    if j == 2:
                        V.wait_ge(lg_done, (N + 1) * RQ)
                        link(V.tensor_scalar(lgb[:, :, :], lg[:, :, :], 1.0, None, ALU.mult))
                        link(V.tensor_reduce(m1[:, :], lgb[:, :, :], AX_X, ALU.max))
                        V.tensor_tensor(lm[:, :, :], lgb[:, :, :], each(m1[:, :], NE), ALU.subtract).then_inc(lm_done, 1)
                        first_of(link, lgb[:, :, :], m1[:, :], oh[:, :, :])
                    elif j == 3:
                        link(V.scalar_tensor_tensor(l2[:, :, :], oh[:, :, :], NEVER, lgb[:, :, :], ALU.mult, ALU.add))
                        link(V.tensor_reduce(m1[:, :], l2[:, :, :], AX_X, ALU.max))
                        first_of(link, l2[:, :, :], m1[:, :], sel[:, :, :])
                    elif j == 0:
                        link(V.tensor_tensor(sel[:, :, :], sel[:, :, :], oh[:, :, :], ALU.add))
                        link(V.tensor_tensor(tmp8[:, :, :], sel[:, :, :], along(pow2, RG), ALU.mult))
                        link(V.tensor_reduce(code[:, :], tmp8[:, :, :], AX_X, ALU.add))
                        V.tensor_tensor(pc[:, 0:RG * NPAIR].rearrange("p (g c) -> p g c", g=RG), along(pairconst, RG),
                                        each(code[:, :], NPAIR), ALU.is_equal).then_inc(pc_done, 1)
                        V.wait_ge(EX_done, N + 1)
                        link(V.tensor_tensor(tmp8[:, :, :], sel[:, :, :], EX[:, :, :], ALU.mult))
                        link(V.tensor_reduce(den[:, :], (EX if l else tmp8)[:, :, :], AX_X, ALU.add))
                    else:
                        link(V.reciprocal(den[:, :], den[:, :]))
                        link(V.tensor_tensor(cw[:, :, :], tmp8[:, :, :], each(den[:, :], NE), ALU.mult))
                        link(V.tensor_tensor(cwh[:, :, :], along(pow2x2, RG), each(code[:, :], NE), ALU.is_gt))
                        link(V.tensor_tensor(cwh[:, :, :], cwh[:, :, :], cw[:, :, :], ALU.mult))
                        link(V.tensor_reduce(wpair[:, :, 1], cwh[:, :, :], AX_X, ALU.add))
                        link(V.tensor_tensor(cw[:, :, :], cw[:, :, :], cwh[:, :, :], ALU.subtract))
                        link(V.tensor_reduce(wpair[:, :, 0], cw[:, :, :], AX_X, ALU.add))
                        V.tensor_scalar(xcols_of_batch(b, P + 2, P + 4), wpair[:, :, :], 1.0, None, ALU.mult)

                def xcols_of_batch(b, lo, hi):
                    if isinstance(b, int):
                        return X[:, RG * b:RG * b + RG, lo:hi]
                    return X[:, bass.ds(b * RG, RG), lo:hi]

                def place(t, j, B):
                    if j != 2 or not there(t, 14, NQ):
                        return
                    b = B - 3
                    N = l * NB + b
                    link = linker(placing, N * PLACE_LINKS, PLACE_LINKS)
                    dve.wait_ge(ranks_done, N + 1)
                    ranks = G_[:, 0:RG * NPAIR].rearrange("p (g c) -> p g c", g=RG)
                    link(dve.tensor_tensor(slm[:, :, :], ranks, along(base[:, :], RG), ALU.add))
                    link(dve.tensor_tensor(slm[:, :, :], slm[:, :, :],
                                           pc[:, 0:RG * NPAIR].rearrange("p (g c) -> p g c", g=RG), ALU.mult))
                    link(dve.tensor_reduce(slotf[:, :], slm[:, :, :], AX_X, ALU.add))
                    dve.tensor_scalar(of_batch(idx_rows[l], b), slotf[:, :], 1.0, None, ALU.mult)
                    dve.tensor_tensor(base[:, :], base[:, :], G_[:, RG * NPAIR:(RG + 1) * NPAIR],
                                      ALU.add).then_inc(slots_done, 1)

                def step(t, j, B):
                    if l == 0:
                        invert_sums(t, j)
                        maxima(t, j, 0)
                        weigh(t, j)
                        negated_leaky_max(t, j, 0)
                        norm_moments(t, j, B)
                        leaky(t, j, 0)
                        add_positive(t, j)
                        take_logits(t, j)
                        residual(t, j)
                        place(t, j, B)
                        choose(t, j, B)
                    else:
                        late = later(l, t, j, B)
                        for u in range(4):
                            if u == 1:
                                invert_sums(*late[0:2])
                            leaky(t, j, u)
                            maxima(t, j, u)
                            if u == 0:
                                take_logits(*late[0:2])
                            elif u == 1:
                                weigh(*late[0:2])
                            elif u == 2:
                                add_positive(*late[0:2])
                            else:
                                residual(*late[0:2])
                            negated_leaky_max(t, j, u)
                            if u == 0:
                                norm_moments(t, j, B)
                            elif u == 1:
                                place(*late)
                            elif u == 2:
                                choose(*late)

                def pack_b2():
                    link = linker(packed, l * PACK_LINKS, PACK_LINKS)
                    dve.wait_ge(b2_in, 16 * (l + 1))
                    for k in range(3):
                        link(dve.tensor_copy(b2_part[:, k, :], b2_rows[:, :]))
                        if k < 2:
                            link(dve.tensor_tensor(b2_rows[:, :], b2_rows[:, :], b2_part[:, k, :], ALU.subtract))
                    link(dve.tensor_scalar(b2_rows[:, :], b2_part[:, 0, :], ident[0:3, 0:1], None, ALU.mult))
                    link(dve.scalar_tensor_tensor(b2_rows[:, :], b2_part[:, 1, :], ident[0:3, 1:2], b2_rows[:, :],
                                                ALU.mult, ALU.add))
                    link(dve.scalar_tensor_tensor(experts[0:3, :, LAST:PACK].bitcast(BF16),
                                                b2_part[:, 2, :].rearrange("p (e d) -> p e d", e=NE), ident[0:3, 2:3],
                                                b2_rows[:, :].rearrange("p (e d) -> p e d", e=NE), ALU.mult, ALU.add))

                if l:
                    dve.wait_ge(padded, 16 * (NPAIR + 1))
                dve.tensor_copy(base[:, :], region).then_inc(base_reset, 1)
                dve.wait_ge(base_reset, l + 1)
                attention_steps(dve, step, 11 + l)

                link = linker(plan, l * PLAN_LINKS, PLAN_LINKS)
                V = dve
                V.wait_ge(slots_done, (l + 1) * NB)
                link(V.tensor_copy(base_i[:, :], base[:, :]))
                link(V.tensor_tensor(cnt[:, :], base[:, :], region, ALU.subtract))
                link(V.tensor_scalar(cnt_i[:, :], cnt[:, :], float(P - 1), None, ALU.add))
                link(V.tensor_scalar(cnt_j[:, :], cnt_i[:, :], P.bit_length() - 1, None, ALU.arith_shift_right))
                link(V.tensor_copy(ntile[:, :], cnt_j[:, :]))
                link(V.tensor_tensor_scan(cum[:, :], ones_pair[:, :], ntile[:, :], 0.0, ALU.mult, ALU.add))
                link(V.tensor_tensor(shift[:, :], cum[:, :], ntile[:, :], ALU.subtract))
                link(V.scalar_tensor_tensor(shift[:, :], shift[:, :], float(P), region, ALU.mult, ALU.subtract))
                link(V.tensor_tensor(le[:, :, :], along(cum[:, :], 2), each(tile_no[:, :], NPAIR), ALU.is_le))
                for k, grow in enumerate((grow_region, grow_lower, grow_upper, ntile[:, :])):
                    link(V.tensor_tensor(lx[:, :, :], le[:, :, :], along(grow, 2), ALU.mult))
                    link(V.tensor_reduce(tvals[:, :, k] if k < 3 else tstart[:, :], lx[:, :, :], AX_X, ALU.add))
                link(V.tensor_scalar(tvals[:, :, 2], tvals[:, :, 2], 1.0, None, ALU.add))
                link(V.tensor_tensor(tvalid[:, :], cum[:, NPAIR - 1:NPAIR].to_broadcast([P, 2]), tile_no[:, :],
                                     ALU.is_gt))
                link(V.tensor_tensor(tstart[:, :], tile_no[:, :], tstart[:, :], ALU.subtract))
                link(V.tensor_tensor(tstart[:, :], tstart[:, :], tvalid[:, :], ALU.mult))
                V.scalar_tensor_tensor(tvals[:, :, 0], tstart[:, :], float(P), tvals[:, :, 0], ALU.mult,
                                       ALU.add).then_inc(tvals_done, 1)
                V.wait_ge(tableT_done, l + 1)
                V.tensor_copy(table[:, :], T_[0:3, 0:TB]).then_inc(table_done, 1)

                pack_b2()
                V.wait_ge(experts_in, 16 * 3 * NE * (l + 1))
                V.wait_ge(table_done, l + 1)

                def tile(t, j, b):
                    T = NT * l + t
                    if there(t, 0, NT):
                        col = slice(t, t + 1) if isinstance(t, int) else bass.ds(t, 1)
                        held(xs_in[j], (b + (in_slot(j, TQ) * l + 1)) * 16)
                        expert = dve.value_load(table[1:2, col], min_val=0, max_val=NE - 1)
                        dve.tensor_scalar(xsn[j % 4][:, :], xs[j][:, 0:P], xs[j][:, P:P + 1], xs[j][:, P + 1:P + 2],
                                          ALU.subtract, ALU.mult).then_inc(xsn_done, 1)
                        dve.tensor_copy(wst[j % 4][:, 0, :], experts[:, bass.ds(expert, 1), :].rearrange(
                            "p a c -> p (a c)")).then_inc(staged, 1)
                    if there(t, 3, NT):
                        k = (j - 3) % 4
                        row = xs[(j - 3) % TQ]
                        wait(dve, y_out[k], (b * 2 + ((j - 3) // 4 + in_slot(k, 4) * l)) * 16)
                        dve.wait_ge(y_done, T - 2)
                        dve.scalar_tensor_tensor(ya[k % 2][:, :], Y_[k % 2][:, 0:P], row[:, P + 2:P + 3],
                                                 row[:, 0:P], ALU.mult, ALU.add).then_inc(ya_done, 1)
                        dve.wait_ge(ya_done, T - 2)
                        dve.scalar_tensor_tensor(yo[k][:, :], Y_[k % 2][:, P:2 * P], row[:, P + 3:P + 4],
                                                 ya[k % 2][:, :], ALU.mult, ALU.add).then_inc(yo_done, 1)

                tile_steps(dve, tile, 3)


def shape_constants(np, n_graphs):
    cap = n_graphs * P + P
    e = np.arange(NE)
    lo, hi = np.array(PAIRS).T
    region = np.arange(NPAIR) * cap
    grow = [np.diff(np.append(v, end)) for v, end in ((region, NPAIR * cap), (lo, 0), (hi, 1))]
    return np.concatenate([NE - e, 2.0 ** e, 2.0 ** (e + 1), 2.0 ** lo + 2.0 ** hi, region, *grow]).astype(np.float32)


_INS = ['x', 'adj', 'L0_gnn_W', 'L0_gnn_a', 'L0_ffn_Wg', 'L0_ffn_bg', 'L0_ffn_bias', 'L0_ffn_W1', 'L0_ffn_b1',
        'L0_ffn_W2', 'L0_ffn_b2', 'L1_gnn_W', 'L1_gnn_a', 'L1_ffn_gate_w', 'L1_ffn_gate_b', 'L1_ffn_W1',
        'L1_ffn_b1', 'L1_ffn_W2', 'L1_ffn_b2']


def build_from(nc, ap, out):
    build_program(nc, ap['x'], ap['adj'], (ap['L0_gnn_W'], ap['L1_gnn_W']), (ap['L0_gnn_a'], ap['L1_gnn_a']),
                  (ap['L0_ffn_Wg'], ap['L1_ffn_gate_w']), (ap['L0_ffn_bg'], ap['L0_ffn_bias'], ap['L1_ffn_gate_b']),
                  (ap['L0_ffn_W1'], ap['L1_ffn_W1']), (ap['L0_ffn_b1'], ap['L1_ffn_b1']),
                  (ap['L0_ffn_W2'], ap['L1_ffn_W2']), (ap['L0_ffn_b2'], ap['L1_ffn_b2']), ap['consts'], out)


def kernel(**inputs):
    import numpy as _np
    import concourse.bacc as _bacc
    from concourse import mybir as _mybir
    from concourse.bass_utils import run_bass_kernel_spmd as _run

    nc = _bacc.Bacc("TRN2", target_bir_lowering=False, num_devices=1)
    arrays, aps = {}, {}
    given = {name: _np.ascontiguousarray(inputs[name]) for name in _INS}
    given['consts'] = shape_constants(_np, given['x'].shape[0])
    for name, a in given.items():
        arrays[f"in_{name}_dram"] = a
        aps[name] = nc.dram_tensor(f"in_{name}_dram", a.shape, _mybir.dt.from_np(a.dtype), kind="ExternalInput").ap()
    out = nc.dram_tensor("out_dram", given['x'].shape, F32, kind="ExternalOutput").ap()
    build_from(nc, aps, out)
    r = _run(nc, [arrays], core_ids=[0])
    return r.results[0]["out_dram"]
```
